# Optimizing a Trainium2 kernel written in Bass

```python
import numpy as np
import jax
import jax.numpy as jnp

def _softmax(x, axis=-1):
    return jax.nn.softmax(x, axis=axis)

def _gelu(x):
    return jax.nn.gelu(x, approximate=True)

def _silu(x):
    return jax.nn.silu(x)

def _sigmoid(x):
    return jax.nn.sigmoid(x)

def _layernorm(x, axis=-1, eps=1e-05):
    m = jnp.mean(x, axis=axis, keepdims=True)
    v = jnp.var(x, axis=axis, keepdims=True)
    return (x - m) / jnp.sqrt(v + eps)

def _scatter_add(tgt, idx, src, axis=0):
    return tgt.at[idx].add(src)

def _segment_sum(src, seg, n):
    return jax.ops.segment_sum(src, seg, n)
kernel_name = 'mk_cond_resid_d2_seqx_r8_14b6c7'

def setup_inputs(seed: int=0):
    np.random.seed(seed)
    _w = jnp.asarray

    def _rec_inputs():
        import jax
        import jax.numpy as jnp
        _rk = jax.random.key(seed)
        x = -0.000125 + 0.9999 * jax.random.normal(jax.random.fold_in(_rk, 1), (64, 32, 512), jnp.float32)
        _lenS = 32 - jax.random.randint(jax.random.fold_in(_rk, 7), (64,), 0, max(1, 32 // 4) + 1, jnp.int32)
        _lenS2 = 32 - jax.random.randint(jax.random.fold_in(_rk, 8), (64,), 0, max(1, 32 // 4) + 1, jnp.int32)
        itok_B_6_15 = jax.random.randint(jax.random.fold_in(_rk, 11), (64,), 6, 16, jnp.int32)
        itok_B_3_7 = jax.random.randint(jax.random.fold_in(_rk, 12), (64,), 3, 8, jnp.int32)
        return (x, itok_B_6_15, itok_B_3_7)
    x, itok_B_6_15, itok_B_3_7 = _rec_inputs()

    def _L0_cond_setup():
        import jax, jax.numpy as jnp
        import numpy as np
        B, S, D_IN, D_OUT = (4, 256, 512, 512)
        RANK, MAX_LORAS = (16, 32)
        key = jax.random.key(seed)
        ks = jax.random.split(key, 6)
        x = jax.random.normal(ks[0], (B, S, D_IN), dtype=jnp.float32)
        adapter_ids = jax.random.randint(ks[1], (B,), 0, MAX_LORAS)
        base_weight = jax.random.normal(ks[2], (D_OUT, D_IN), dtype=jnp.float32) * D_IN ** (-0.5)
        base_bias = jax.random.normal(ks[3], (D_OUT,), dtype=jnp.float32) * 0.01
        lora_A_w = jax.random.normal(ks[4], (MAX_LORAS, RANK, D_IN), dtype=jnp.float32) * D_IN ** (-0.5)
        lora_B_w = jax.random.normal(ks[5], (MAX_LORAS, D_OUT, RANK), dtype=jnp.float32) * RANK ** (-0.5)
        return {'x': x, 'adapter_ids': adapter_ids, 'base_weight': base_weight, 'base_bias': base_bias, 'lora_A_w': lora_A_w, 'lora_B_w': lora_B_w}
    _L0_cond_all = _L0_cond_setup()
    _L0_cond_in = {k: v for k, v in _L0_cond_all.items() if k in ('base_weight', 'base_bias', 'lora_A_w', 'lora_B_w')}
    del _L0_cond_all

    def _L1_cond_setup():
        import jax, jax.numpy as jnp
        import numpy as np
        RANK = 16
        ALPHA = 16.0
        SCALING = ALPHA / RANK
        N_ADAPTERS = 8
        IN_F = 512
        OUT_F = 512
        BATCH = 4
        SEQ = 256
        key = jax.random.key(seed)
        kx, ka, kb, ki = jax.random.split(key, 4)
        x = jax.random.normal(kx, (BATCH, SEQ, IN_F), dtype=jnp.float32)
        A = jax.random.normal(ka, (N_ADAPTERS, OUT_F, RANK), dtype=jnp.float32) * 0.02
        B = jax.random.normal(kb, (N_ADAPTERS, RANK, IN_F), dtype=jnp.float32) * 0.02
        adapter_ids = jax.random.randint(ki, (BATCH,), 0, N_ADAPTERS, dtype=jnp.int32)
        return {'x': x, 'A': A, 'B': B, 'adapter_ids': adapter_ids}
    _L1_cond_all = _L1_cond_setup()
    _L1_cond_in = {k: v for k, v in _L1_cond_all.items() if k in ('A', 'B')}
    del _L1_cond_all
    return {'x': x, 'itok_B_6_15': itok_B_6_15, 'itok_B_3_7': itok_B_3_7, 'L0_cond_base_weight': _L0_cond_in['base_weight'], 'L0_cond_base_bias': _L0_cond_in['base_bias'], 'L0_cond_lora_A_w': _L0_cond_in['lora_A_w'], 'L0_cond_lora_B_w': _L0_cond_in['lora_B_w'], 'L1_cond_A': _L1_cond_in['A'], 'L1_cond_B': _L1_cond_in['B']}

def reference(x, itok_B_6_15, itok_B_3_7, L0_cond_base_weight, L0_cond_base_bias, L0_cond_lora_A_w, L0_cond_lora_B_w, L1_cond_A, L1_cond_B):
    import jax
    import jax.numpy as jnp

    def _L0_cond_ref(x, adapter_ids, base_weight, base_bias, lora_A_w, lora_B_w):
        import jax, jax.numpy as jnp
        import numpy as np
        B, S, D_IN, D_OUT = (4, 256, 512, 512)
        RANK, MAX_LORAS = (16, 32)
        result = jnp.einsum('bsd,od->bso', x, base_weight) + base_bias
        A = lora_A_w[adapter_ids]
        Bw = lora_B_w[adapter_ids]
        h = jnp.einsum('bsd,brd->bsr', x, A)
        lora_out = jnp.einsum('bsr,bor->bso', h, Bw)
        result = result + lora_out
        return result.astype(x.dtype)

    def _L1_cond_ref(x, A, B, adapter_ids):
        import jax, jax.numpy as jnp
        import numpy as np
        RANK = 16
        ALPHA = 16.0
        SCALING = ALPHA / RANK
        N_ADAPTERS = 8
        IN_F = 512
        OUT_F = 512
        BATCH = 4
        SEQ = 256
        B_sel = B[adapter_ids]
        A_sel = A[adapter_ids]
        Bx = jnp.einsum('bni,bri->bnr', x, B_sel)
        out = jnp.einsum('bnr,bor->bno', Bx, A_sel)
        return out * SCALING
    x = x + _L0_cond_ref(x, itok_B_6_15, L0_cond_base_weight, L0_cond_base_bias, L0_cond_lora_A_w, L0_cond_lora_B_w)
    x = x + _L1_cond_ref(x, L1_cond_A, L1_cond_B, itok_B_3_7)
    return x

_drawn_inputs = setup_inputs


def setup_inputs(seed=0):
    import zlib

    import numpy as np

    out = dict(_drawn_inputs(seed))
    spreads = {}
    factors = {'L0_cond_base_bias': 8.0}
    for name, (base, spread) in spreads.items():
        noise = np.random.default_rng([zlib.crc32(name.encode()), seed]).standard_normal(out[name].shape)
        drawn = base * np.exp(spread * noise) if base else spread * noise
        out[name] = jnp.asarray(drawn.astype(out[name].dtype))
    for name, factor in factors.items():
        out[name] = (out[name] * factor).astype(out[name].dtype)
    return out
```

```python
from contextlib import ExitStack

import concourse.bass as bass
from concourse import mybir

F32 = mybir.dt.float32
F32R = mybir.dt.float32r
I32 = mybir.dt.int32
ALU = mybir.AluOpType
ACT = mybir.ActivationFunctionType

P = 128
B, S, D = 64, 32, 512
R = 16
N0, N1 = 32, 8
C = D // P
NB = P // S
NBLK = B * S // P
PAIRS = NBLK // 2
L0, L1 = 0, 1
UP, DOWN = 0, 1


def two_lora_layers(nc, x, ids0, ids1, weight, bias, lora_a, lora_b, l1_a, l1_b, out):
    x_blocks = x.rearrange("(k a) s d -> k (a s) d", a=NB)
    out_blocks = out.rearrange("(k a) s d -> k (a s) d", a=NB)

    ctx = ExitStack()
    with ctx:
        def sb(name, shape, dtype=F32):
            return ctx.enter_context(nc.sbuf_tensor(name, shape, dtype))

        def sem(name):
            return ctx.enter_context(nc.semaphore(name))

        ids = sb("ids", [1, 2 * B], I32)
        w_rows = sb("w_rows", [P, C, D])
        a_rows = sb("a_rows", [P, C, D])
        bw_rows = sb("bw_rows", [P, P, R])
        a1_rows = sb("a1_rows", [N1 * C, P, R])
        b1_rows = sb("b1_rows", [P, D])
        bias_rows = sb("bias_rows", [C, P])
        bias_all = sb("bias_all", [P, D])
        x_in = sb("x_in", [P, 2, D])
        ident = sb("ident", [P, P])
        batch_mask = sb("batch_mask", [P, NB, S])
        g_mask = sb("g_mask", [P, NB + 1, R])
        wt_hi = sb("wt_hi", [P, C, D], F32R)
        wt_lo = sb("wt_lo", [P, C, D], F32R)
        table0_rounded = sb("table0_rounded", [P, N0, 2, C, R], F32R)
        table1_rounded = sb("table1_rounded", [P, N1, 2, C, R], F32R)
        table0_exact = sb("table0_exact", [P, N0, C, R])
        table1_exact = sb("table1_exact", [P, N1, 2, C, R])
        c1_sum = sb("c1_sum", [P, C, P])
        sel_rounded = sb("sel_rounded", [P, 2, 2, C, NB, 2, R], F32R)
        sel_exact = sb("sel_exact", [P, 2, 2, C, NB + 1, 2, R])
        xt_hi = sb("xt_hi", [P, 2, C, P], F32R)
        xt_lo = sb("xt_lo", [P, 2, C, P], F32R)
        up_rows = sb("up_rows", [P, 2, D])
        g_sel = sb("g_sel", [P, 2, NB + 1, 2, R])
        h_all = sb("h_all", [P, 2, P])
        u_sel = sb("u_sel", [P, 2, P])
        y = sb("y", [P, 2, D])

        banks = [ctx.enter_context(nc.psum_tensor(f"bank{i}", [P, D], F32)) for i in range(8)]
        XT, RT, G, U, OUT0, OUT1 = 0, 1, 2, 3, 4, 5

        ids_in, w_in, a_in, bw_in = sem("ids_in"), sem("w_in"), sem("a_in"), sem("bw_in")
        a1_in, b1_in, bias_in, bias_all_in = sem("a1_in"), sem("b1_in"), sem("bias_in"), sem("bias_all_in")
        x_loaded = [sem("x_loaded_even"), sem("x_loaded_odd")]
        y_stored = [sem("y_stored_even"), sem("y_stored_odd")]
        pool_step, zeros_ready = sem("pool_step"), sem("zeros_ready")
        ident_ready, masks_ready = sem("ident_ready"), sem("masks_ready")
        filled = sem("filled")
        act_drained = sem("act_drained")
        dve_drained = sem("dve_drained")
        c1_summed, c1_lo_ready = sem("c1_summed"), sem("c1_lo_ready")
        bias_ready = sem("bias_ready")
        xt_filled = sem("xt_filled")
        up_filled = sem("up_filled")
        g_filled = sem("g_filled")
        u_filled = sem("u_filled")
        gh_filled = sem("gh_filled")
        out_filled = sem("out_filled")
        xt_hi_ready, xt_lo_ready = sem("xt_hi_ready"), sem("xt_lo_ready")
        up_ready, h_ready, g_ready, u_ready = sem("up_ready"), sem("h_ready"), sem("g_ready"), sem("u_ready")
        y_ready, xb_ready = sem("y_ready"), sem("xb_ready")
        rounded_ready, exact_ready = sem("rounded_ready"), sem("exact_ready")

        BIAS_FILL, B1_FILL, W_FILL, C1_FILL, A1_FILL, BW_FILL, A_FILL, FILLS = 0, 1, 2, 6, 7, 8, 12, 16

        BY_ACT = [f for f in range(FILLS) if f not in (B1_FILL, BW_FILL, BW_FILL + 2)]
        BY_DVE = [f for f in range(1, FILLS) if f not in (A1_FILL, BW_FILL + 1, BW_FILL + 3)]

        def bank(f):
            return banks[f % 8]

        def wait_drained(engine, f):
            engine.wait_ge(act_drained, sum(g <= f for g in BY_ACT))
            if f >= BY_DVE[0]:
                engine.wait_ge(dve_drained, sum(g <= f for g in BY_DVE))

        block = ctx.enter_context(nc.Block())

        @block.sync
        def _(sp):
            sp.dma_start(b1_rows[:, :], l1_b.rearrange("n r d -> (n r) d")).then_inc(b1_in, 16)
            sp.dma_start(w_rows[:, :, :], weight.rearrange("(c p) d -> p c d", p=P)).then_inc(w_in, 16)
            sp.dma_start(a1_rows[:, :, :], l1_a.rearrange("n (c p) r -> (n c) p r", p=P)).then_inc(a1_in, 16)
            sp.dma_start(bw_rows[:, :, :], lora_b.rearrange("n (c p) r -> (n c) p r", p=P)).then_inc(bw_in, 16)
            sp.dma_start(x_in[:, 0, :], x_blocks[0, :, :]).then_inc(x_loaded[0], 16)
            sp.dma_start(a_rows[:, :, :], lora_a.rearrange("(g n) r d -> (n r) g d", g=C)).then_inc(a_in, 16)
            sp.dma_start(x_in[:, 1, :], x_blocks[1, :, :]).then_inc(x_loaded[1], 16)

            def load(k, slot):
                sp.wait_ge(xt_filled, k - 1)
                sp.wait_ge(xb_ready, k - 1)
                sp.dma_start(x_in[:, slot, :], x_blocks[k, :, :]).then_inc(x_loaded[slot], 16)

            def store(k, slot):
                sp.wait_ge(y_ready, k + 1)
                sp.dma_start(out_blocks[k, :, :], y[:, slot, :]).then_inc(y_stored[slot], 16)

            with sp.Fori(0, PAIRS - 1) as i:
                for s in range(2):
                    load(i * 2 + (s + 2), s)
                    store(i * 2 + s, s)
            for s in range(2):
                store(NBLK - 2 + s, s)
            for s in range(2):
                sp.wait_ge(y_stored[s], 16 * (NBLK // 2))

        @block.gpsimd
        def _(pool):
            nc.gpsimd.memset(ident[:, :], 0.0).then_inc(pool_step, 1)
            nc.gpsimd.memset(batch_mask[:, :, :], 1.0).then_inc(pool_step, 1)
            nc.gpsimd.memset(g_mask[:, :, :], 1.0).then_inc(pool_step, 1)
            nc.gpsimd.memset(g_sel[:, :, :, :, :], 0.0).then_inc(zeros_ready, 1)
            for s in range(2):
                nc.gpsimd.memset(sel_exact[:, s, DOWN, :, NB, :, :], 0.0).then_inc(zeros_ready, 1)
            pool.wait_ge(pool_step, 3)
            nc.gpsimd.affine_select(out=ident[:, :], in_=ident[:, :], compare_op=ALU.not_equal, fill=1.0,
                                    base=0, pattern=[[-1, P]], channel_multiplier=1).then_inc(ident_ready, 1)
            nc.gpsimd.affine_select(out=batch_mask[:, :, :], in_=batch_mask[:, :, :], compare_op=ALU.is_ge,
                                    fill=0.0, base=0, pattern=[[-S, NB], [0, S]],
                                    channel_multiplier=1).then_inc(pool_step, 1)
            nc.gpsimd.affine_select(out=g_mask[:, 0:NB, :], in_=g_mask[:, 0:NB, :], compare_op=ALU.is_ge,
                                    fill=0.0, base=0, pattern=[[-2 * R, NB], [0, R]],
                                    channel_multiplier=1).then_inc(pool_step, 1)
            pool.wait_ge(pool_step, 5)
            nc.gpsimd.affine_select(out=batch_mask[:, :, :], in_=batch_mask[:, :, :], compare_op=ALU.is_ge,
                                    fill=0.0, base=S - 1, pattern=[[S, NB], [0, S]],
                                    channel_multiplier=-1).then_inc(masks_ready, 1)
            nc.gpsimd.affine_select(out=g_mask[:, 0:NB, :], in_=g_mask[:, 0:NB, :], compare_op=ALU.is_ge,
                                    fill=0.0, base=R - 1, pattern=[[2 * R, NB], [0, R]],
                                    channel_multiplier=-1).then_inc(pool_step, 1)
            pool.wait_ge(pool_step, 6)
            for b in range(NB):
                nc.gpsimd.tensor_tensor(out=g_mask[:, NB, :], in0=g_mask[:, NB, :], in1=g_mask[:, b, :],
                                        op=ALU.subtract).then_inc(pool_step if b < NB - 1 else masks_ready, 1)
                if b < NB - 1:
                    pool.wait_ge(pool_step, 7 + b)

            def add_bias(pair, slot, wait_store=None):
                pool.wait_ge(x_loaded[slot], pair * 16 + 16)
                if wait_store is not None:
                    pool.wait_ge(y_stored[slot], wait_store)
                nc.gpsimd.tensor_tensor(out=y[:, slot, :], in0=x_in[:, slot, :], in1=bias_all[:, :],
                                        op=ALU.add).then_inc(xb_ready, 1)

            def select(k, slot, reads=None):
                if reads is not None:
                    pool.wait_ge(g_filled, reads)
                for b in range(NB):
                    n0 = pool.value_load(ids[0:1, bass.ds(k * NB + b, 1)], min_val=0, max_val=N0 - 1)
                    for place in (UP, DOWN):
                        nc.gpsimd.tensor_copy(sel_exact[:, slot, place, :, b, L0, :],
                                              table0_exact[:, bass.ds(n0, 1), :, :])
                    n1 = pool.value_load(ids[0:1, bass.ds(k * NB + B + b, 1)], min_val=0, max_val=N1 - 1)
                    last = nc.gpsimd.tensor_copy(sel_exact[:, slot, :, :, b, L1, :],
                                                 table1_exact[:, bass.ds(n1, 1), :, :, :])
                last.then_inc(exact_ready, 1)

            pool.wait_ge(ids_in, 32)
            pool.wait_ge(bias_all_in, 16)
            wait_drained(pool, A_FILL - 1)
            pool.wait_ge(c1_lo_ready, 1)
            for k in range(2):
                select(k, k)
                add_bias(0, k)
            with pool.Fori(1, PAIRS) as i:
                for s in range(2):
                    select(i * 2 + s, s, reads=i * 2 + (s - 1))
                    add_bias(i, s, wait_store=i * 16)

        @block.tensor
        def _(pe):
            def fill_room(f):
                if f >= 8:
                    wait_drained(pe, f - 8)

            pe.wait_ge(ident_ready, 1)
            pe.wait_ge(bias_in, 16)
            nc.tensor.transpose(bank(BIAS_FILL)[:, 0:C], bias_rows[:, :], ident[0:C, 0:C]).then_inc(filled, 1)
            pe.wait_ge(b1_in, 16)
            for c in range(C):
                last = nc.tensor.transpose(bank(B1_FILL)[:, c * P:(c + 1) * P], b1_rows[:, c * P:(c + 1) * P],
                                           ident[:, :])
            last.then_inc(filled, 1)
            pe.wait_ge(w_in, 16)
            for c in range(C):
                for oc in range(C):
                    last = nc.tensor.transpose(bank(W_FILL + c)[:, oc * P:(oc + 1) * P],
                                               w_rows[:, oc, c * P:(c + 1) * P], ident[:, :])
                last.then_inc(filled, 1)
            wait_drained(pe, B1_FILL)
            for c in range(C):
                for oc in range(C):
                    last = nc.tensor.matmul(bank(C1_FILL)[:, c * P:(c + 1) * P], w_rows[:, oc, c * P:(c + 1) * P],
                                            table1_exact[:, :, 1, oc, :], start=(oc == 0), stop=(oc == C - 1))
            last.then_inc(filled, 1)
            pe.wait_ge(a1_in, 16)
            for r in range(R):
                last = nc.tensor.transpose(bank(A1_FILL)[:, r * N1 * C:(r + 1) * N1 * C], a1_rows[:, :, r],
                                           ident[0:N1 * C, 0:N1 * C])
            last.then_inc(filled, 1)
            pe.wait_ge(bw_in, 16)
            for q in range(4):
                fill_room(BW_FILL + q)
                for r in range(4):
                    last = nc.tensor.transpose(bank(BW_FILL + q)[:, r * P:(r + 1) * P], bw_rows[:, :, 4 * q + r],
                                               ident[:, :])
                last.then_inc(filled, 1)
            pe.wait_ge(a_in, 16)
            for g in range(4):
                fill_room(A_FILL + g)
                for c in range(C):
                    last = nc.tensor.transpose(bank(A_FILL + g)[:, c * P:(c + 1) * P],
                                               a_rows[:, g, c * P:(c + 1) * P], ident[:, :])
                last.then_inc(filled, 1)

            def transpose_x(pair, slot):
                pe.wait_ge(x_loaded[slot], pair * 16 + 16)
                for c in range(C):
                    last = nc.tensor.transpose(banks[XT][:, c * P:(c + 1) * P], x_in[:, slot, c * P:(c + 1) * P],
                                               ident[:, :])
                last.then_inc(xt_filled, 1)

            def base(k, slot, chunks):
                dst = banks[OUT0 + slot][:, :]
                for c in chunks:
                    for n, (xs, ws) in enumerate(((xt_hi, wt_hi), (xt_hi, wt_lo), (xt_lo, wt_hi))):
                        nc.tensor.matmul(dst, xs[:, slot, c, :], ws[:, c, :], start=(c == 0 and n == 0), stop=False)

            def exact_stage(k, slot, free=True):
                pe.wait_ge(exact_ready, k + 1)
                if free:
                    pe.wait_ge(up_ready, k)
                    pe.wait_ge(g_ready, k)
                for c in range(C):
                    last = nc.tensor.transpose(banks[RT][:, c * P:(c + 1) * P],
                                               sel_exact[:, slot, UP, c, 0:NB, :, :], ident[:, :])
                last.then_inc(up_filled, 1)
                for c in range(C):
                    last = nc.tensor.matmul(banks[G][:, 0:(NB + 1) * R], sel_exact[:, slot, DOWN, c, 0:NB, :, :],
                                            sel_exact[:, slot, DOWN, c, :, L1, :],
                                            start=(c == 0), stop=(c == C - 1))
                last.then_inc(g_filled, 1)

            def down(k, slot, free=True):
                pe.wait_ge(xt_hi_ready, k + 1)
                pe.wait_ge(xt_lo_ready, k + 1)
                pe.wait_ge(rounded_ready, k + 1)
                n = 0
                for c in range(C):
                    for part, xs in ((0, xt_hi), (1, xt_hi), (0, xt_lo)):
                        last = nc.tensor.matmul(banks[U][:, 0:P],
                                                sel_rounded[:, slot, part, c, :, :, :],
                                                xs[:, slot, c, :], start=(n == 0), stop=(n == 3 * C - 1))
                        n += 1
                last.then_inc(u_filled, 1)

            def add_gh(k, slot):
                pe.wait_ge(h_ready, k + 1)
                pe.wait_ge(g_ready, k + 1)
                nc.tensor.matmul(banks[U][:, 0:P], g_sel[:, slot, 0:NB, :, :], h_all[:, slot, :],
                                 start=False, stop=True, skip_group_check=True).then_inc(gh_filled, 1)

            def up(k, slot):
                pe.wait_ge(up_ready, k + 1)
                pe.wait_ge(u_ready, k + 1)
                nc.tensor.matmul(banks[OUT0 + slot][:, :], u_sel[:, slot, :], up_rows[:, slot, :],
                                 start=False, stop=True).then_inc(out_filled, 1)

            def step(pair, slot, y_free=True, ahead=True):
                k = pair * 2 + slot
                if ahead:
                    transpose_x(pair + slot, 1 - slot)
                add_gh(k, slot)
                if y_free:
                    pe.wait_ge(y_ready, k - 1)
                base(k, slot, range(0, C // 2))
                if ahead:
                    exact_stage(k + 1, 1 - slot)
                base(k, slot, range(C // 2, C))
                up(k, slot)
                if ahead:
                    down(k + 1, 1 - slot)

            wait_drained(pe, FILLS - 1)
            pe.wait_ge(c1_lo_ready, 1)
            pe.wait_ge(bias_ready, 2)
            transpose_x(0, 0)
            exact_stage(0, 0, free=False)
            down(0, 0)
            step(0, 0, y_free=False)
            step(0, 1, y_free=False)
            with pe.Fori(1, PAIRS - 1) as i:
                step(i, 0)
                step(i, 1)
            step(PAIRS - 1, 0)
            step(PAIRS - 1, 1, ahead=False)

        def by_adapter(fill, n):
            return bank(fill)[:, :].rearrange("p (c n r) -> p n c r", c=C, n=n)

        def by_rank(fill, n):
            return bank(fill)[:, :].rearrange("p (r n c) -> p n c r", n=n, c=C)

        @block.scalar
        def _(act):
            act.dma_start(ids[0:1, 0:B], ids0.rearrange("(a n) -> a n", a=1)).then_inc(ids_in, 16)
            act.dma_start(ids[0:1, B:2 * B], ids1.rearrange("(a n) -> a n", a=1)).then_inc(ids_in, 16)
            act.dma_start(bias_rows[:, :], bias.rearrange("(c p) -> c p", p=P)).then_inc(bias_in, 16)
            act.dma_start(bias_all[:, :], bias.rearrange("(a n) -> a n", a=1).to_broadcast([P, D])).then_inc(bias_all_in, 16)

            def copy(dst, src):
                return nc.scalar.activation(dst, src, ACT.Copy)

            act.wait_ge(zeros_ready, 3)
            act.wait_ge(filled, BIAS_FILL + 1)
            for s in range(2):
                last = copy(sel_exact[:, s, DOWN, :, NB, L1, 0], bank(BIAS_FILL)[:, 0:C])
                last.then_inc(bias_ready, 1)
            act.wait_ge(bias_ready, 2)
            act.sem_inc(act_drained, 1)
            for c in range(C):
                act.wait_ge(filled, W_FILL + c + 1)
                copy(wt_hi[:, c, :], bank(W_FILL + c)[:, :]).then_inc(act_drained, 1)
            act.wait_ge(c1_summed, 1)
            copy(table1_rounded[:, :, 0, :, :],
                 c1_sum[:, :, :].rearrange("p c (n r) -> p n c r", r=R)).then_inc(act_drained, 1)
            act.wait_ge(filled, A1_FILL + 1)
            copy(table1_exact[:, :, 0, :, :], by_rank(A1_FILL, N1)).then_inc(act_drained, 1)
            for q in (1, 3):
                act.wait_ge(filled, BW_FILL + q + 1)
                copy(table0_exact[:, :, :, 4 * q:4 * q + 4], by_rank(BW_FILL + q, N0)).then_inc(act_drained, 1)
            for g in range(4):
                act.wait_ge(filled, A_FILL + g + 1)
                copy(table0_rounded[:, g * 8:g * 8 + 8, 0, :, :], by_adapter(A_FILL + g, 8)).then_inc(act_drained, 1)

            def xt_high(k, slot, free=True):
                act.wait_ge(xt_filled, k + 1)
                if free:
                    act.wait_ge(out_filled, k - 1)
                copy(xt_hi[:, slot, :, :], banks[XT][:, :].rearrange("p (c m) -> p c m", c=C)).then_inc(xt_hi_ready, 1)

            def up_copy(k, slot):
                act.wait_ge(up_filled, k + 1)
                copy(up_rows[:, slot, :], banks[RT][:, :]).then_inc(up_ready, 1)

            def h_copy(k, slot):
                act.wait_ge(u_filled, k + 1)
                copy(h_all[:, slot, :], banks[U][:, 0:P]).then_inc(h_ready, 1)

            def step(k, slot, free=True):
                h_copy(k, slot)
                xt_high(k + 1, 1 - slot, free)
                up_copy(k + 1, 1 - slot)

            xt_high(0, 0, free=False)
            up_copy(0, 0)
            step(0, 0, free=False)
            with act.Fori(0, PAIRS - 1) as i:
                step(i * 2 + 1, 1)
                step(i * 2 + 2, 0)
            h_copy(NBLK - 1, 1)

        @block.vector
        def _(dve):
            dve.wait_ge(filled, B1_FILL + 1)
            nc.vector.tensor_copy(table1_exact[:, :, 1, :, :], by_adapter(B1_FILL, N1)).then_inc(dve_drained, 1)

            def low(dst, whole, high):
                return nc.vector.tensor_tensor(out=dst, in0=whole, in1=high, op=ALU.subtract)

            for c in range(C):
                dve.wait_ge(act_drained, sum(g <= W_FILL + c for g in BY_ACT))
                low(wt_lo[:, c, :], bank(W_FILL + c)[:, :], wt_hi[:, c, :]).then_inc(dve_drained, 1)
            dve.wait_ge(filled, C1_FILL + 1)
            dve.wait_ge(dve_drained, 1)
            nc.vector.tensor_tensor(out=c1_sum[:, :, :].rearrange("p c (n r) -> p c n r", r=R),
                                    in0=bank(C1_FILL)[:, :].rearrange("p (c n r) -> p c n r", c=C, r=R),
                                    in1=table1_exact[:, :, 1, :, :].rearrange("p n c r -> p c n r"),
                                    op=ALU.add).then_inc(c1_summed, 1)
            dve.wait_ge(c1_summed, 1)
            dve.wait_ge(act_drained, sum(g <= C1_FILL for g in BY_ACT))
            low(table1_rounded[:, :, 1, :, :], c1_sum[:, :, :].rearrange("p c (n r) -> p n c r", r=R),
                table1_rounded[:, :, 0, :, :]).then_inc(c1_lo_ready, 1)
            dve.wait_ge(c1_lo_ready, 1)
            dve.sem_inc(dve_drained, 1)
            for q in (0, 2):
                dve.wait_ge(filled, BW_FILL + q + 1)
                nc.vector.tensor_copy(table0_exact[:, :, :, 4 * q:4 * q + 4],
                                      by_rank(BW_FILL + q, N0)).then_inc(dve_drained, 1)
            for g in range(4):
                dve.wait_ge(act_drained, sum(h <= A_FILL + g for h in BY_ACT))
                low(table0_rounded[:, g * 8:g * 8 + 8, 1, :, :], by_adapter(A_FILL + g, 8),
                    table0_rounded[:, g * 8:g * 8 + 8, 0, :, :]).then_inc(dve_drained, 1)
            dve.wait_ge(dve_drained, len(BY_DVE))
            wait_drained(dve, FILLS - 1)
            dve.wait_ge(ids_in, 32)
            dve.wait_ge(masks_ready, 2)

            def select(k, slot, free=True):
                if free:
                    dve.wait_ge(u_filled, k - 1)
                for b in range(NB):
                    n0 = dve.value_load(ids[0:1, bass.ds(k * NB + b, 1)], min_val=0, max_val=N0 - 1)
                    nc.vector.tensor_copy(sel_rounded[:, slot, :, :, b, L0, :],
                                          table0_rounded[:, bass.ds(n0, 1), :, :, :])
                    n1 = dve.value_load(ids[0:1, bass.ds(k * NB + B + b, 1)], min_val=0, max_val=N1 - 1)
                    last = nc.vector.tensor_copy(sel_rounded[:, slot, :, :, b, L1, :],
                                                 table1_rounded[:, bass.ds(n1, 1), :, :, :])
                last.then_inc(rounded_ready, 1)

            def xt_low(k, slot):
                dve.wait_ge(xt_hi_ready, k + 1)
                low(xt_lo[:, slot, :, :], banks[XT][:, :].rearrange("p (c m) -> p c m", c=C),
                    xt_hi[:, slot, :, :]).then_inc(xt_lo_ready, 1)

            def g_masked(k, slot):
                dve.wait_ge(g_filled, k + 1)
                nc.vector.tensor_tensor(out=g_sel[:, slot, :, 1, :],
                                        in0=banks[G][:, 0:(NB + 1) * R].rearrange("p (b r) -> p b r", r=R),
                                        in1=g_mask[:, :, :], op=ALU.mult).then_inc(g_ready, 1)

            def u_masked(k, slot):
                dve.wait_ge(gh_filled, k + 1)
                dve.wait_ge(g_ready, k + 1)
                nc.vector.scalar_tensor_tensor(out=u_sel[:, slot, :], in0=banks[U][:, 0:P],
                                               scalar=g_sel[:, slot, NB, 1, 0:1],
                                               in1=batch_mask[:, :, :].rearrange("p b s -> p (b s)"),
                                               op0=ALU.add, op1=ALU.mult).then_inc(u_ready, 1)

            def finish(k, slot):
                dve.wait_ge(out_filled, k + 1)
                dve.wait_ge(xb_ready, k + 1)
                nc.vector.tensor_tensor(out=y[:, slot, :], in0=banks[OUT0 + slot][:, :], in1=y[:, slot, :],
                                        op=ALU.add).then_inc(y_ready, 1)

            def step(k, slot, before=True, ahead=True, free=True):
                if before:
                    finish(k - 1, 1 - slot)
                u_masked(k, slot)
                if ahead:
                    xt_low(k + 1, 1 - slot)
                    select(k + 1, 1 - slot, free)
                    g_masked(k + 1, 1 - slot)

            select(0, 0, free=False)
            xt_low(0, 0)
            g_masked(0, 0)
            step(0, 0, before=False, free=False)
            with dve.Fori(0, PAIRS - 1) as i:
                step(i * 2 + 1, 1)
                step(i * 2 + 2, 0)
            step(NBLK - 1, 1, ahead=False)
            finish(NBLK - 1, 1)


_INPUTS = ["x", "itok_B_6_15", "itok_B_3_7", "L0_cond_base_weight", "L0_cond_base_bias",
           "L0_cond_lora_A_w", "L0_cond_lora_B_w", "L1_cond_A", "L1_cond_B"]


def kernel(**inputs):
    import numpy as np
    import concourse.bacc as bacc
    from concourse.bass_utils import run_bass_kernel_spmd

    nc = bacc.Bacc("TRN2", target_bir_lowering=False, num_devices=1)
    arrays, args = {}, []
    for name in _INPUTS:
        a = np.ascontiguousarray(inputs[name])
        arrays[f"in_{name}"] = a
        args.append(nc.dram_tensor(f"in_{name}", a.shape, mybir.dt.from_np(a.dtype), kind="ExternalInput").ap())
    out = nc.dram_tensor("out", (B, S, D), F32, kind="ExternalOutput").ap()
    two_lora_layers(nc, *args, out)
    return run_bass_kernel_spmd(nc, [arrays], core_ids=[0]).results[0]["out"]
```

```python
from contextlib import ExitStack

import concourse.bass as bass
from concourse import mybir

F32 = mybir.dt.float32
F32R = mybir.dt.float32r
I32 = mybir.dt.int32
ALU = mybir.AluOpType
ACT = mybir.ActivationFunctionType

P = 128
B, S, D = 64, 32, 512
R = 16
N0, N1 = 32, 8
C = D // P
NB = P // S
NBLK = B * S // P
PAIRS = NBLK // 2
L0, L1 = 0, 1
HI, LO = 0, 1


def two_lora_layers(nc, x, ids0, ids1, weight, bias, lora_a, lora_b, l1_a, l1_b, out):
    x_blocks = x.rearrange("(k a) s d -> k (a s) d", a=NB)
    out_blocks = out.rearrange("(k a) s d -> k (a s) d", a=NB)

    ctx = ExitStack()
    with ctx:
        def sb(name, shape, dtype=F32):
            return ctx.enter_context(nc.sbuf_tensor(name, shape, dtype))

        def sem(name):
            return ctx.enter_context(nc.semaphore(name))

        ids = sb("ids", [1, NBLK, 2, NB], I32)
        w_rows = sb("w_rows", [P, C, D])
        a_rows = sb("a_rows", [P, C, D])
        bw_rows = sb("bw_rows", [P, P, R])
        a1_rows = sb("a1_rows", [N1 * C, P, R])
        b1_rows = sb("b1_rows", [P, D])
        bias_all = sb("bias_all", [P, D])
        x_in = sb("x_in", [P, 2, D])
        ident = sb("ident", [P, P])
        batch_mask = sb("batch_mask", [P, NB, S])
        g_mask = sb("g_mask", [P, NB + 1, R])
        first_ranks = sb("first_ranks", [P, NB, R])
        wt_hi = sb("wt_hi", [P, C, D], F32R)
        wt_lo = sb("wt_lo", [P, C, D], F32R)
        table0_rounded = sb("table0_rounded", [P, N0, 2, C, R], F32R)
        table1_rounded = sb("table1_rounded", [P, N1, 2, C, R], F32R)
        table0_exact = sb("table0_exact", [P, N0, C + 1, R])
        table1_exact = sb("table1_exact", [P, N1, C + 1, R])
        b1_cols = sb("b1_cols", [P, C, P])
        c1_sum = sb("c1_sum", [P, C, P])
        bias_b1 = sb("bias_b1", [P, 1])
        bias_b1_terms = sb("bias_b1_terms", [P, D])
        sel_rounded = sb("sel_rounded", [P, 2, 2, C, NB, 2, R], F32R)
        sel_exact = sb("sel_exact", [P, 2, C + 1, NB + 1, 2, R])
        xt = sb("xt", [P, 2, C, 2, P], F32R)
        up_rows = sb("up_rows", [P, 2, D])
        g_sel = sb("g_sel", [P, 2, NB + 1, 2, R])
        u_lo_part = sb("u_lo_part", [P, P])
        u_all = sb("u_all", [P, P])
        u_sel = sb("u_sel", [P, 2, P])
        y = sb("y", [P, 2, D])

        banks = [ctx.enter_context(nc.psum_tensor(f"bank{i}", [P, D], F32)) for i in range(8)]
        XT, RT, G, U, OUT0, OUT1 = 0, 1, 2, 3, 4, 5

        ids_in, w_in, a_in, bw_in = sem("ids_in"), sem("w_in"), sem("a_in"), sem("bw_in")
        a1_in, b1_in, bias_all_in = sem("a1_in"), sem("b1_in"), sem("bias_all_in")
        x_loaded = [sem("x_loaded_even"), sem("x_loaded_odd")]
        y_stored = [sem("y_stored_even"), sem("y_stored_odd")]
        pool_step, zeros_ready = sem("pool_step"), sem("zeros_ready")
        ident_ready, masks_ready = sem("ident_ready"), sem("masks_ready")
        ident_copied = sem("ident_copied")
        filled = sem("filled")
        act_drained = sem("act_drained")
        dve_drained = sem("dve_drained")
        c1_summed, c1_lo_ready = sem("c1_summed"), sem("c1_lo_ready")
        bias_b1_step, bias_b1_ready = sem("bias_b1_step"), sem("bias_b1_ready")
        xt_filled = sem("xt_filled")
        up_filled = sem("up_filled")
        g_filled = sem("g_filled")
        u_filled = sem("u_filled")
        gh_filled = sem("gh_filled")
        out_filled = sem("out_filled")
        xt_hi_ready, xt_lo_ready = sem("xt_hi_ready"), sem("xt_lo_ready")
        up_ready, g_ready = sem("up_ready"), sem("g_ready")
        u_lo_ready, u_all_ready, u_ready = sem("u_lo_ready"), sem("u_all_ready"), sem("u_ready")
        y_ready, xb_ready = sem("y_ready"), sem("xb_ready")
        rounded_ready, exact_ready = sem("rounded_ready"), sem("exact_ready")

        B1_FILL, W_FILL, C1_FILL, A1_FILL, BW_FILL, G_FILL, A_FILL, FILLS = 0, 1, 5, 6, 7, 11, 12, 16

        BY_ACT = [f for f in range(FILLS) if f not in (B1_FILL, BW_FILL, BW_FILL + 2)]
        BY_DVE = [f for f in range(FILLS) if f not in (A1_FILL, BW_FILL + 1, BW_FILL + 3, G_FILL)]

        def bank(f):
            return banks[f % 8]

        def wait_drained(engine, f):
            engine.wait_ge(dve_drained, sum(g <= f for g in BY_DVE))
            if f >= BY_ACT[0]:
                engine.wait_ge(act_drained, sum(g <= f for g in BY_ACT))

        block = ctx.enter_context(nc.Block())

        @block.sync
        def _(sp):
            sp.dma_start(b1_rows[:, :], l1_b.rearrange("n r d -> (n r) d")).then_inc(b1_in, 16)
            sp.dma_start(w_rows[:, :, :], weight.rearrange("(c p) d -> p c d", p=P)).then_inc(w_in, 16)
            sp.dma_start(a1_rows[:, :, :], l1_a.rearrange("n (c p) r -> (n c) p r", p=P)).then_inc(a1_in, 16)
            sp.dma_start(bw_rows[:, :, :], lora_b.rearrange("n (c p) r -> (n c) p r", p=P)).then_inc(bw_in, 16)
            sp.dma_start(x_in[:, 0, :], x_blocks[0, :, :]).then_inc(x_loaded[0], 16)
            sp.dma_start(a_rows[:, :, :], lora_a.rearrange("(g n) r d -> (n r) g d", g=C)).then_inc(a_in, 16)
            sp.dma_start(x_in[:, 1, :], x_blocks[1, :, :]).then_inc(x_loaded[1], 16)

            def load(k, slot):
                sp.wait_ge(xt_filled, k - 1)
                sp.wait_ge(xb_ready, k - 1)
                sp.dma_start(x_in[:, slot, :], x_blocks[k, :, :]).then_inc(x_loaded[slot], 16)

            def store(k, slot):
                sp.wait_ge(y_ready, k + 1)
                sp.dma_start(out_blocks[k, :, :], y[:, slot, :]).then_inc(y_stored[slot], 16)

            with sp.Fori(0, PAIRS - 1) as i:
                for s in range(2):
                    load(i * 2 + (s + 2), s)
                    store(i * 2 + s, s)
            for s in range(2):
                store(NBLK - 2 + s, s)
            for s in range(2):
                sp.wait_ge(y_stored[s], 16 * (NBLK // 2))

        @block.gpsimd
        def _(pool):
            nc.gpsimd.memset(ident[:, :], 0.0).then_inc(pool_step, 1)
            nc.gpsimd.memset(batch_mask[:, :, :], 1.0).then_inc(pool_step, 1)
            nc.gpsimd.memset(g_mask[:, :, :], 1.0).then_inc(pool_step, 1)
            nc.gpsimd.memset(first_ranks[:, :, :], 1.0).then_inc(pool_step, 1)
            nc.gpsimd.memset(g_sel[:, :, :, :, :], 0.0).then_inc(pool_step, 1)
            nc.gpsimd.memset(sel_exact[:, :, C, NB, :, :], 0.0).then_inc(zeros_ready, 1)
            pool.wait_ge(pool_step, 5)
            nc.gpsimd.affine_select(out=ident[:, :], in_=ident[:, :], compare_op=ALU.not_equal, fill=1.0,
                                    base=0, pattern=[[-1, P]], channel_multiplier=1).then_inc(ident_ready, 1)
            for s in range(2):
                nc.gpsimd.affine_select(out=g_sel[:, s, 0:NB, L0, :], in_=g_sel[:, s, 0:NB, L0, :],
                                        compare_op=ALU.not_equal, fill=1.0, base=0,
                                        pattern=[[-2 * R, NB], [-1, R]],
                                        channel_multiplier=1).then_inc(zeros_ready, 1)
            bands = ((batch_mask[:, :, :], S, S), (g_mask[:, 0:NB, :], R, 2 * R), (first_ranks[:, :, :], R, R))
            for band, columns, height in bands:
                nc.gpsimd.affine_select(out=band, in_=band, compare_op=ALU.is_ge, fill=0.0, base=0,
                                        pattern=[[-S, NB], [0, columns]], channel_multiplier=1).then_inc(pool_step, 1)
            pool.wait_ge(pool_step, 8)
            for band, columns, height in bands:
                nc.gpsimd.affine_select(out=band, in_=band, compare_op=ALU.is_ge, fill=0.0, base=height - 1,
                                        pattern=[[S, NB], [0, columns]], channel_multiplier=-1).then_inc(pool_step, 1)
            pool.wait_ge(pool_step, 11)
            for b in range(NB):
                nc.gpsimd.tensor_tensor(out=g_mask[:, NB, :], in0=g_mask[:, NB, :], in1=first_ranks[:, b, :],
                                        op=ALU.subtract).then_inc(pool_step, 1)
                pool.wait_ge(pool_step, 12 + b)
            pool.sem_inc(masks_ready, 1)

            def add_bias(pair, slot, wait_store=None):
                pool.wait_ge(x_loaded[slot], pair * 16 + 16)
                if wait_store is not None:
                    pool.wait_ge(y_stored[slot], wait_store)
                nc.gpsimd.tensor_tensor(out=y[:, slot, :], in0=x_in[:, slot, :], in1=bias_all[:, :],
                                        op=ALU.add).then_inc(xb_ready, 1)

            pool.wait_ge(bias_all_in, 16)
            for s in range(2):
                add_bias(0, s)
            with pool.Fori(1, PAIRS) as i:
                for s in range(2):
                    add_bias(i, s, wait_store=i * 16)

        def adapters_of(engine, k):
            loads = []
            for layer, n in ((L0, N0), (L1, N1)):
                _, values = nc.values_load_multi_w_load_instructions(
                    ids[0:1, bass.ds(k, 1), layer, :], engines=[engine.engine], min_val=0, max_val=n - 1,
                    skip_runtime_bounds_check_because="the inputs index the adapter tables")
                loads.append(values)
            return loads

        @block.tensor
        def _(pe):
            def fill_room(f):
                if f >= 8:
                    wait_drained(pe, f - 8)

            pe.wait_ge(ident_ready, 1)
            pe.wait_ge(b1_in, 16)
            for c in range(C):
                last = nc.tensor.transpose(bank(B1_FILL)[:, c * P:(c + 1) * P], b1_rows[:, c * P:(c + 1) * P],
                                           ident[:, :])
            last.then_inc(filled, 1)
            pe.wait_ge(w_in, 16)
            for c in range(C):
                for oc in range(C):
                    last = nc.tensor.transpose(bank(W_FILL + c)[:, oc * P:(oc + 1) * P],
                                               w_rows[:, oc, c * P:(c + 1) * P], ident[:, :])
                last.then_inc(filled, 1)
            wait_drained(pe, B1_FILL)
            for c in range(C):
                for oc in range(C):
                    last = nc.tensor.matmul(bank(C1_FILL)[:, c * P:(c + 1) * P], w_rows[:, oc, c * P:(c + 1) * P],
                                            b1_cols[:, oc, :], start=(oc == 0), stop=(oc == C - 1))
            last.then_inc(filled, 1)
            pe.wait_ge(a1_in, 16)
            for r in range(R):
                last = nc.tensor.transpose(bank(A1_FILL)[:, r * N1 * C:(r + 1) * N1 * C], a1_rows[:, :, r],
                                           ident[0:N1 * C, 0:N1 * C])
            last.then_inc(filled, 1)
            pe.wait_ge(bw_in, 16)
            for q in range(4):
                fill_room(BW_FILL + q)
                for r in range(4):
                    last = nc.tensor.transpose(bank(BW_FILL + q)[:, r * P:(r + 1) * P], bw_rows[:, :, 4 * q + r],
                                               ident[:, :])
                last.then_inc(filled, 1)
            fill_room(G_FILL)
            wait_drained(pe, G_FILL - 1)
            for oc in range(C):
                last = nc.tensor.matmul(bank(G_FILL)[:, :], b1_cols[:, oc, :], table0_exact[:, :, oc, :],
                                        start=(oc == 0), stop=(oc == C - 1))
            last.then_inc(filled, 1)
            pe.wait_ge(a_in, 16)
            for g in range(4):
                fill_room(A_FILL + g)
                for c in range(C):
                    last = nc.tensor.transpose(bank(A_FILL + g)[:, c * P:(c + 1) * P],
                                               a_rows[:, g, c * P:(c + 1) * P], ident[:, :])
                last.then_inc(filled, 1)

            def transpose_x(pair, slot):
                pe.wait_ge(x_loaded[slot], pair * 16 + 16)
                for c in range(C):
                    last = nc.tensor.transpose(banks[XT][:, c * P:(c + 1) * P], x_in[:, slot, c * P:(c + 1) * P],
                                               ident[:, :])
                last.then_inc(xt_filled, 1)

            def base(k, slot, chunks):
                dst = banks[OUT0 + slot][:, :]
                for c in chunks:
                    for n, (part, ws) in enumerate(((HI, wt_hi), (HI, wt_lo), (LO, wt_hi))):
                        nc.tensor.matmul(dst, xt[:, slot, c, part, :], ws[:, c, :], start=(c == 0 and n == 0), stop=False)

            def exact_stage(k, slot, free=True):
                pe.wait_ge(exact_ready, k + 1)
                if free:
                    pe.wait_ge(up_ready, k)
                    pe.wait_ge(g_ready, k)
                for c in range(C):
                    last = nc.tensor.transpose(banks[RT][:, c * P:(c + 1) * P],
                                               sel_exact[:, slot, c, 0:NB, :, :], ident[:, :])
                last.then_inc(up_filled, 1)
                nc.tensor.matmul(banks[G][:, 0:(NB + 1) * R], sel_exact[:, slot, C, 0:NB, :, :],
                                 sel_exact[:, slot, C, :, L1, :], start=True, stop=True).then_inc(g_filled, 1)

            def down(k, slot):
                pe.wait_ge(xt_hi_ready, k + 1)
                pe.wait_ge(xt_lo_ready, k + 1)
                pe.wait_ge(rounded_ready, k + 1)
                for c in range(C):
                    nc.tensor.matmul(banks[U][:, 0:2 * P], sel_rounded[:, slot, HI, c, :, :, :],
                                     xt[:, slot, c, :, :], start=(c == 0), stop=False)
                    last = nc.tensor.matmul(banks[U][:, 0:P], sel_rounded[:, slot, LO, c, :, :, :],
                                            xt[:, slot, c, HI, :], start=False, stop=(c == C - 1))
                last.then_inc(u_filled, 1)

            def add_gh(k, slot):
                pe.wait_ge(u_all_ready, k + 1)
                nc.tensor.matmul(banks[U][:, 2 * P:3 * P], g_sel[:, slot, 0:NB, :, :], u_all[:, :],
                                 start=True, stop=True).then_inc(gh_filled, 1)

            def up(k, slot):
                pe.wait_ge(up_ready, k + 1)
                pe.wait_ge(u_ready, k + 1)
                nc.tensor.matmul(banks[OUT0 + slot][:, :], u_sel[:, slot, :], up_rows[:, slot, :],
                                 start=False, stop=True).then_inc(out_filled, 1)

            def step(pair, slot, y_free=True, ahead=True):
                k = pair * 2 + slot
                if ahead:
                    transpose_x(pair + slot, 1 - slot)
                if y_free:
                    pe.wait_ge(y_ready, k - 1)
                base(k, slot, range(0, C // 2))
                add_gh(k, slot)
                if ahead:
                    exact_stage(k + 1, 1 - slot)
                base(k, slot, range(C // 2, C))
                up(k, slot)
                if ahead:
                    down(k + 1, 1 - slot)

            wait_drained(pe, FILLS - 1)
            pe.wait_ge(c1_lo_ready, 1)
            pe.wait_ge(bias_b1_ready, 2)
            pe.wait_ge(zeros_ready, 3)
            transpose_x(0, 0)
            exact_stage(0, 0, free=False)
            down(0, 0)
            step(0, 0, y_free=False)
            step(0, 1, y_free=False)
            with pe.Fori(1, PAIRS - 1) as i:
                step(i, 0)
                step(i, 1)
            step(PAIRS - 1, 0)
            step(PAIRS - 1, 1, ahead=False)

        def by_adapter(fill, n):
            return bank(fill)[:, :].rearrange("p (c n r) -> p n c r", c=C, n=n)

        def by_rank(fill, n):
            return bank(fill)[:, :].rearrange("p (r n c) -> p n c r", n=n, c=C)

        @block.scalar
        def _(act):
            for layer, ids_of in ((L0, ids0), (L1, ids1)):
                act.dma_start(ids[0:1, :, layer, :],
                              ids_of.rearrange("(a k b) -> a k b", a=1, b=NB)).then_inc(ids_in, 16)
            act.dma_start(bias_all[:, :], bias.rearrange("(a n) -> a n", a=1).to_broadcast([P, D])).then_inc(bias_all_in, 16)

            def copy(dst, src):
                return nc.scalar.activation(dst, src, ACT.Copy)

            act.wait_ge(ident_ready, 1)
            copy(table1_exact[:, :, C, :], ident[:, :].rearrange("p (n r) -> p n r", r=R)).then_inc(ident_copied, 1)
            for c in range(C):
                act.wait_ge(filled, W_FILL + c + 1)
                copy(wt_hi[:, c, :], bank(W_FILL + c)[:, :]).then_inc(act_drained, 1)
            act.wait_ge(c1_summed, 1)
            copy(table1_rounded[:, :, 0, :, :],
                 c1_sum[:, :, :].rearrange("p c (n r) -> p n c r", r=R)).then_inc(act_drained, 1)
            act.wait_ge(filled, A1_FILL + 1)
            copy(table1_exact[:, :, 0:C, :], by_rank(A1_FILL, N1)).then_inc(act_drained, 1)
            for q in (1, 3):
                act.wait_ge(filled, BW_FILL + q + 1)
                copy(table0_exact[:, :, 0:C, 4 * q:4 * q + 4], by_rank(BW_FILL + q, N0)).then_inc(act_drained, 1)
            act.wait_ge(filled, G_FILL + 1)
            copy(table0_exact[:, :, C, :], bank(G_FILL)[:, :].rearrange("p (n r) -> p n r", r=R)).then_inc(act_drained, 1)
            for g in range(4):
                act.wait_ge(filled, A_FILL + g + 1)
                copy(table0_rounded[:, g * 8:g * 8 + 8, 0, :, :], by_adapter(A_FILL + g, 8)).then_inc(act_drained, 1)

            def xt_high(k, slot, free=True):
                act.wait_ge(xt_filled, k + 1)
                if free:
                    act.wait_ge(out_filled, k - 1)
                copy(xt[:, slot, :, HI, :], banks[XT][:, :].rearrange("p (c m) -> p c m", c=C)).then_inc(xt_hi_ready, 1)

            def select(k, slot, free=True):
                if free:
                    act.wait_ge(g_filled, k - 1)
                n0, n1 = adapters_of(act, k)
                for b in range(NB):
                    copy(sel_exact[:, slot, :, b, L0, :], table0_exact[:, bass.ds(n0[b], 1), :, :])
                    last = copy(sel_exact[:, slot, :, b, L1, :], table1_exact[:, bass.ds(n1[b], 1), :, :])
                last.then_inc(exact_ready, 1)

            def up_copy(k, slot):
                act.wait_ge(up_filled, k + 1)
                copy(up_rows[:, slot, :], banks[RT][:, :]).then_inc(up_ready, 1)

            def u_low(k, slot):
                act.wait_ge(u_filled, k + 1)
                act.wait_ge(g_ready, k + 1)
                nc.scalar.activation(u_lo_part[:, :], banks[U][:, P:2 * P], ACT.Identity,
                                     bias=g_sel[:, slot, NB, L1, 0:1]).then_inc(u_lo_ready, 1)

            def step(k, slot, free=True):
                u_low(k, slot)
                xt_high(k + 1, 1 - slot, free)
                select(k + 1, 1 - slot, free)
                up_copy(k + 1, 1 - slot)

            act.wait_ge(ids_in, 32)
            act.wait_ge(ident_copied, 1)
            wait_drained(act, FILLS - 1)
            select(0, 0, free=False)
            xt_high(0, 0, free=False)
            up_copy(0, 0)
            step(0, 0, free=False)
            with act.Fori(0, PAIRS - 1) as i:
                step(i * 2 + 1, 1)
                step(i * 2 + 2, 0)
            u_low(NBLK - 1, 1)

        @block.vector
        def _(dve):
            dve.wait_ge(filled, B1_FILL + 1)
            nc.vector.tensor_copy(b1_cols[:, :, :],
                                  bank(B1_FILL)[:, :].rearrange("p (c m) -> p c m", c=C)).then_inc(dve_drained, 1)

            def low(dst, whole, high):
                return nc.vector.tensor_tensor(out=dst, in0=whole, in1=high, op=ALU.subtract)

            for c in range(C):
                dve.wait_ge(act_drained, sum(g <= W_FILL + c for g in BY_ACT))
                low(wt_lo[:, c, :], bank(W_FILL + c)[:, :], wt_hi[:, c, :]).then_inc(dve_drained, 1)
            dve.wait_ge(filled, C1_FILL + 1)
            dve.wait_ge(dve_drained, 1)
            nc.vector.tensor_tensor(out=c1_sum[:, :, :], in0=bank(C1_FILL)[:, :].rearrange("p (c m) -> p c m", c=C),
                                    in1=b1_cols[:, :, :], op=ALU.add).then_inc(c1_summed, 1)
            dve.wait_ge(c1_summed, 1)
            dve.wait_ge(act_drained, sum(g <= C1_FILL for g in BY_ACT))
            low(table1_rounded[:, :, 1, :, :], c1_sum[:, :, :].rearrange("p c (n r) -> p n c r", r=R),
                table1_rounded[:, :, 0, :, :]).then_inc(c1_lo_ready, 1)
            dve.wait_ge(c1_lo_ready, 1)
            dve.sem_inc(dve_drained, 1)
            for q in (0, 2):
                dve.wait_ge(filled, BW_FILL + q + 1)
                nc.vector.tensor_copy(table0_exact[:, :, 0:C, 4 * q:4 * q + 4],
                                      by_rank(BW_FILL + q, N0)).then_inc(dve_drained, 1)
            for g in range(4):
                dve.wait_ge(act_drained, sum(h <= A_FILL + g for h in BY_ACT))
                low(table0_rounded[:, g * 8:g * 8 + 8, 1, :, :], by_adapter(A_FILL + g, 8),
                    table0_rounded[:, g * 8:g * 8 + 8, 0, :, :]).then_inc(dve_drained, 1)
            dve.wait_ge(dve_drained, len(BY_DVE))
            wait_drained(dve, FILLS - 1)
            dve.wait_ge(ids_in, 32)
            dve.wait_ge(bias_all_in, 16)
            dve.wait_ge(b1_in, 16)
            nc.vector.tensor_tensor(out=bias_b1_terms[:, :], in0=b1_rows[:, :], in1=bias_all[:, :],
                                    op=ALU.mult).then_inc(bias_b1_step, 1)
            dve.wait_ge(bias_b1_step, 1)
            nc.vector.reduce_sum(bias_b1[:, :], bias_b1_terms[:, :], axis=mybir.AxisListType.X).then_inc(bias_b1_step, 1)
            dve.wait_ge(bias_b1_step, 2)
            dve.wait_ge(zeros_ready, 1)
            for s in range(2):
                nc.vector.tensor_copy(sel_exact[:, s, C, NB, L1, 0:1], bias_b1[:, :]).then_inc(bias_b1_ready, 1)
            dve.wait_ge(masks_ready, 1)

            def select(k, slot, free=True):
                if free:
                    dve.wait_ge(u_filled, k - 1)
                n0, n1 = adapters_of(dve, k)
                for b in range(NB):
                    nc.vector.tensor_copy(sel_rounded[:, slot, :, :, b, L0, :],
                                          table0_rounded[:, bass.ds(n0[b], 1), :, :, :])
                    last = nc.vector.tensor_copy(sel_rounded[:, slot, :, :, b, L1, :],
                                                 table1_rounded[:, bass.ds(n1[b], 1), :, :, :])
                last.then_inc(rounded_ready, 1)

            def xt_low(k, slot):
                dve.wait_ge(xt_hi_ready, k + 1)
                low(xt[:, slot, :, LO, :], banks[XT][:, :].rearrange("p (c m) -> p c m", c=C),
                    xt[:, slot, :, HI, :]).then_inc(xt_lo_ready, 1)

            def g_masked(k, slot):
                dve.wait_ge(g_filled, k + 1)
                nc.vector.tensor_tensor(out=g_sel[:, slot, :, L1, :],
                                        in0=banks[G][:, 0:(NB + 1) * R].rearrange("p (b r) -> p b r", r=R),
                                        in1=g_mask[:, :, :], op=ALU.mult).then_inc(g_ready, 1)

            def u_sum(k, slot):
                dve.wait_ge(u_lo_ready, k + 1)
                nc.vector.tensor_tensor(out=u_all[:, :], in0=banks[U][:, 0:P], in1=u_lo_part[:, :],
                                        op=ALU.add).then_inc(u_all_ready, 1)

            def u_masked(k, slot):
                dve.wait_ge(gh_filled, k + 1)
                nc.vector.tensor_tensor(out=u_sel[:, slot, :], in0=banks[U][:, 2 * P:3 * P],
                                        in1=batch_mask[:, :, :].rearrange("p b s -> p (b s)"),
                                        op=ALU.mult).then_inc(u_ready, 1)

            def finish(k, slot):
                dve.wait_ge(out_filled, k + 1)
                dve.wait_ge(xb_ready, k + 1)
                nc.vector.tensor_tensor(out=y[:, slot, :], in0=banks[OUT0 + slot][:, :], in1=y[:, slot, :],
                                        op=ALU.add).then_inc(y_ready, 1)

            def step(k, slot, before=True, ahead=True, free=True):
                if before:
                    finish(k - 1, 1 - slot)
                u_sum(k, slot)
                if ahead:
                    xt_low(k + 1, 1 - slot)
                u_masked(k, slot)
                if ahead:
                    select(k + 1, 1 - slot, free)
                    g_masked(k + 1, 1 - slot)

            select(0, 0, free=False)
            xt_low(0, 0)
            g_masked(0, 0)
            step(0, 0, before=False, free=False)
            with dve.Fori(0, PAIRS - 1) as i:
                step(i * 2 + 1, 1)
                step(i * 2 + 2, 0)
            step(NBLK - 1, 1, ahead=False)
            finish(NBLK - 1, 1)


_INPUTS = ["x", "itok_B_6_15", "itok_B_3_7", "L0_cond_base_weight", "L0_cond_base_bias",
           "L0_cond_lora_A_w", "L0_cond_lora_B_w", "L1_cond_A", "L1_cond_B"]


def kernel(**inputs):
    import numpy as np
    import concourse.bacc as bacc
    from concourse.bass_utils import run_bass_kernel_spmd

    nc = bacc.Bacc("TRN2", target_bir_lowering=False, num_devices=1)
    arrays, args = {}, []
    for name in _INPUTS:
        a = np.ascontiguousarray(inputs[name])
        arrays[f"in_{name}"] = a
        args.append(nc.dram_tensor(f"in_{name}", a.shape, mybir.dt.from_np(a.dtype), kind="ExternalInput").ap())
    out = nc.dram_tensor("out", (B, S, D), F32, kind="ExternalOutput").ap()
    two_lora_layers(nc, *args, out)
    return run_bass_kernel_spmd(nc, [arrays], core_ids=[0]).results[0]["out"]
```

```python
from contextlib import ExitStack

import concourse.bass as bass
from concourse import mybir

F32 = mybir.dt.float32
F32R = mybir.dt.float32r
I32 = mybir.dt.int32
U32 = mybir.dt.uint32
ALU = mybir.AluOpType
ACT = mybir.ActivationFunctionType

P = 128
B, S, D = 64, 32, 512
R = 16
N0, N1 = 32, 8
C = D // P
NB = P // S
NBLK = B * S // P
PAIRS = NBLK // 2
WARM_UPS = 11
L0, L1 = 0, 1
HI, LO = 0, 1
GROUPS = (N0 + N1) * R // P
G_COL, BB_COL = D, D + P
ROW = BB_COL + 4


def two_lora_layers(nc, x, ids0, ids1, weight, bias, lora_a, lora_b, l1_a, l1_b, out):
    x_blocks = x.rearrange("(k a) s d -> k (a s) d", a=NB)
    out_blocks = out.rearrange("(k a) s d -> k (a s) d", a=NB)

    ctx = ExitStack()
    with ctx:
        def sb(name, shape, dtype=F32):
            return ctx.enter_context(nc.sbuf_tensor(name, shape, dtype))

        def sem(name):
            return ctx.enter_context(nc.semaphore(name))

        ids = sb("ids", [1, NBLK, 2, NB], I32)
        w_rows = sb("w_rows", [P, C, D])
        a_rows = sb("a_rows", [P, C, D])
        bw_rows = sb("bw_rows", [P, P, R])
        a1_rows = sb("a1_rows", [N1 * C, P, R])
        b1_rows = sb("b1_rows", [P, D])
        bias_all = sb("bias_all", [P, D])
        x_in = sb("x_in", [P, 2, D])
        ident = sb("ident", [P, P])
        batch_mask = sb("batch_mask", [P, NB, S])
        wd = sb("wd", [P, 2, C, P + D + P], F32R)
        table0_rounded = sb("table0_rounded", [P, N0, 2, C, R], F32R)
        table1_rounded = sb("table1_rounded", [P, N1, 2, C, R], F32R)
        bw_cols = sb("bw_cols", [P, C, N0 * R])
        b1_cols = sb("b1_cols", [P, C, P])
        c1_sum = sb("c1_sum", [P, C, P])
        bw_by_rank = sb("bw_by_rank", [P, R, P])
        a1_by_rank = sb("a1_by_rank", [N1 * C, R, P])
        row_ends = sb("row_ends", [P, GROUPS, ROW - D])
        ids_all = sb("ids_all", [P, 2, NBLK, NB], I32)
        ids_all_f = sb("ids_all_f", [P, 2, NBLK, NB])
        rank_mask = sb("rank_mask", [P, 2, NB])
        row_of_rank = sb("row_of_rank", [P, 2, NB], I32)
        row_of_rank_f = sb("row_of_rank_f", [P, 2, NB])
        row_terms = sb("row_terms", [P, NBLK, 2, NB])
        row_sums = sb("row_sums", [P, NBLK])
        rows = sb("rows", [P, NBLK], U32)
        rows_now = [sb("rows_now_even", [P, 1], U32), sb("rows_now_odd", [P, 1], U32)]
        bias_b1_terms = sb("bias_b1_terms", [P, D])
        gathered_rows = sb("gathered_rows", [P, 2, ROW])
        xt = sb("xt", [P, 2, C, 2, P], F32R)
        up_rows = sb("up_rows", [P, 2, 2, D], F32R)
        bb_sel = sb("bb_sel", [P, 2, 1])
        g_sel = sb("g_sel", [P, 2, NB, 2, R])
        u_blocks = sb("u_blocks", [P, P])
        u_own = sb("u_own", [P, P])
        u_sel = sb("u_sel", [P, 2, P], F32R)
        warm = sb("warm", [P, P])
        xb = sb("xb", [P, 2, D])
        y = sb("y", [P, 2, D])

        psum = ctx.enter_context(nc.psum_tensor("psum", [P, 8, D], F32))
        banks = [psum[:, i, :] for i in range(8)]
        U, EDGE_U, XT = 4, 5, 7
        HALF = D // 2
        W_LEFT, D_AT, U_AT = (0, P), (P + D, 0), ((1, HALF), (0, 0))

        def products(slot):
            return psum[:, 2 * slot:2 * slot + 2, W_LEFT[slot]:W_LEFT[slot] + HALF]

        def u_of(slot):
            at_bank, left = U_AT[slot]
            return psum[:, 2 * slot + at_bank, left:left + P]

        by_rank_dram = nc.dram_tensor("by_rank", (GROUPS * P, ROW), F32, kind="Internal").ap()

        ids_in, a_in, bw_in = sem("ids_in"), sem("a_in"), sem("bw_in")
        w_in = [sem("w_in_first"), sem("w_in_second")]
        a1_in, b1_in, bias_all_in = sem("a1_in"), sem("b1_in"), sem("bias_all_in")
        ids_all_in, table_stored = sem("ids_all_in"), sem("table_stored")
        x_loaded = [sem("x_loaded_even"), sem("x_loaded_odd")]
        gathered = [sem("gathered_even"), sem("gathered_odd")]
        y_stored = [sem("y_stored_even"), sem("y_stored_odd")]
        pool_step, zeros_ready = sem("pool_step"), sem("zeros_ready")
        ident_ready, masks_ready = sem("ident_ready"), sem("masks_ready")
        act_by_rank_ready, dve_by_rank_ready = sem("act_by_rank_ready"), sem("dve_by_rank_ready")
        rows_step, rows_ready, warm_ready = sem("rows_step"), sem("rows_ready"), sem("warm_ready")
        filled = sem("filled")
        act_drained = sem("act_drained")
        dve_drained = sem("dve_drained")
        c1_summed = sem("c1_summed")
        bias_b1_step, bias_b1_ready = sem("bias_b1_step"), sem("bias_b1_ready")
        xt_filled, u_filled, gh_filled, out_filled = sem("xt_filled"), sem("u_filled"), sem("gh_filled"), sem("out_filled")
        xt_hi_ready, xt_lo_ready = sem("xt_hi_ready"), sem("xt_lo_ready")
        sel0_ready, sel1_ready = sem("sel0_ready"), sem("sel1_ready")
        up_hi_ready, up_ready = sem("up_hi_ready"), sem("up_ready")
        g_ready = sem("g_ready")
        u_blocks_ready, u_own_ready = sem("u_blocks_ready"), sem("u_own_ready")
        u_hi_ready, u_ready = sem("u_hi_ready"), sem("u_ready")
        rows_now_ready, gather_issued = sem("rows_now_ready"), sem("gather_issued")
        y_ready, xb_ready = sem("y_ready"), sem("xb_ready")

        FILL_BANKS = 7
        BW_FILL, B1_FILL, W_FILL, G_FILL, A_FILL, C1_FILL, FILLS = 0, 4, (5, 6, 8, 9), 7, 10, (14, 15), 16

        BY_ACT = [f for f in range(FILLS) if f not in (BW_FILL, BW_FILL + 2, B1_FILL, G_FILL)]
        BY_DVE = [f for f in range(FILLS) if f not in (BW_FILL + 1, BW_FILL + 3)]

        def bank(f):
            return banks[(f + EDGE_U - C1_FILL[0]) % FILL_BANKS]

        def wait_drained(engine, f):
            engine.wait_ge(act_drained, sum(g <= f for g in BY_ACT))
            engine.wait_ge(dve_drained, sum(g <= f for g in BY_DVE))

        block = ctx.enter_context(nc.Block())

        @block.sync
        def _(sp):
            w_view = weight.rearrange("(c p) d -> p c d", p=P)
            half = D // 2
            sp.dma_start(bw_rows[:, :, :], lora_b.rearrange("n (c p) r -> (n c) p r", p=P)).then_inc(bw_in, 16)
            sp.dma_start(b1_rows[:, :], l1_b.rearrange("n r d -> (n r) d")).then_inc(b1_in, 16)
            sp.dma_start(w_rows[:, :, 0:half], w_view[:, :, 0:half]).then_inc(w_in[0], 16)
            sp.dma_start(a1_rows[:, :, :], l1_a.rearrange("n (c p) r -> (n c) p r", p=P)).then_inc(a1_in, 16)
            sp.dma_start(w_rows[:, :, half:D], w_view[:, :, half:D]).then_inc(w_in[1], 16)
            sp.dma_start(bias_all[:, :], bias.rearrange("(a n) -> a n", a=1).to_broadcast([P, D])).then_inc(bias_all_in, 16)
            for layer, ids_of in ((L0, ids0), (L1, ids1)):
                sp.dma_start(ids_all[:, layer, :, :].rearrange("p k b -> p (k b)"),
                             ids_of.rearrange("(a k) -> a k", a=1).to_broadcast([P, B])).then_inc(ids_all_in, 16)
            sp.dma_start(x_in[:, 0, :], x_blocks[0, :, :]).then_inc(x_loaded[0], 16)
            sp.dma_start(a_rows[:, :, :], lora_a.rearrange("(g n) r d -> (n r) g d", g=C)).then_inc(a_in, 16)
            for layer, ids_of in ((L0, ids0), (L1, ids1)):
                sp.dma_start(ids[0:1, :, layer, :],
                             ids_of.rearrange("(a k b) -> a k b", a=1, b=NB)).then_inc(ids_in, 16)

            for n, by_rank_part, row in ((N0, bw_by_rank, 0), (N1, a1_by_rank, N0 * R)):
                done = 1 if n == N0 else 2
                sp.wait_ge(act_by_rank_ready, done)
                sp.wait_ge(dve_by_rank_ready, done)
                for c in range(C):
                    view = by_rank_dram[row:row + n * R, c * P:(c + 1) * P].rearrange("(n r) o -> n r o", r=R)
                    sp.dma_start(view, by_rank_part[bass.ds(c, n, step=C), :, :]).then_inc(table_stored, 16)
            sp.wait_ge(zeros_ready, 2)
            sp.wait_ge(bias_b1_ready, 1)
            wait_drained(sp, G_FILL)
            sp.dma_start(by_rank_dram.rearrange("(g p) c -> p g c", p=P)[:, :, D:ROW], row_ends[:, :, :]).then_inc(table_stored, 16)
            sp.dma_start(x_in[:, 1, :], x_blocks[1, :, :]).then_inc(x_loaded[1], 16)

            def load(k, slot):
                sp.wait_ge(xt_filled, k - 1)
                sp.wait_ge(xb_ready, k - 1)
                sp.dma_start(x_in[:, slot, :], x_blocks[k, :, :]).then_inc(x_loaded[slot], 16)

            def store(k, slot):
                sp.wait_ge(y_ready, k + 1)
                sp.dma_start(out_blocks[k, :, :], y[:, slot, :]).then_inc(y_stored[slot], 16)

            load(2, 0)
            with sp.Fori(0, PAIRS - 2) as i:
                load(i * 2 + 3, 1)
                store(i * 2, 0)
                load(i * 2 + 4, 0)
                store(i * 2 + 1, 1)
            load(NBLK - 1, 1)
            for k in range(NBLK - 4, NBLK - 1):
                store(k, k % 2)
            for half in range(2):
                cols = slice(half * HALF, (half + 1) * HALF)
                sp.wait_ge(y_ready, NBLK + half)
                sp.dma_start(out_blocks[NBLK - 1, :, cols], y[:, 1, cols]).then_inc(y_stored[1], 16)
            sp.wait_ge(y_stored[0], 16 * (NBLK // 2))
            sp.wait_ge(y_stored[1], 16 * (NBLK // 2 + 1))

        @block.gpsimd
        def _(pool):
            nc.gpsimd.memset(ident[:, :], 0.0).then_inc(pool_step, 1)
            nc.gpsimd.memset(g_sel[:, :, :, :, :], 0.0).then_inc(pool_step, 1)
            nc.gpsimd.memset(rank_mask[:, :, :], 1.0).then_inc(pool_step, 1)
            nc.gpsimd.memset(batch_mask[:, :, :], 1.0).then_inc(pool_step, 1)
            pool.wait_ge(pool_step, 4)
            nc.gpsimd.affine_select(out=ident[:, :], in_=ident[:, :], compare_op=ALU.not_equal, fill=1.0,
                                    base=0, pattern=[[-1, P]], channel_multiplier=1).then_inc(ident_ready, 1)
            nc.gpsimd.iota(row_of_rank[:, :, :], pattern=[[(N0 - 1) * R, 2], [-2 * R, NB]], base=0,
                           channel_multiplier=1).then_inc(pool_step, 1)
            bands = ((rank_mask[:, :, :], [[-R, 2], [-2 * R, NB]], [[R, 2], [2 * R, NB]], R),
                     (batch_mask[:, :, :], [[-S, NB], [0, S]], [[S, NB], [0, S]], S))
            for band, below, above, height in bands:
                nc.gpsimd.affine_select(out=band, in_=band, compare_op=ALU.is_ge, fill=0.0, base=0,
                                        pattern=below, channel_multiplier=1).then_inc(pool_step, 1)
            pool.wait_ge(pool_step, 7)
            for band, below, above, height in bands:
                nc.gpsimd.affine_select(out=band, in_=band, compare_op=ALU.is_ge, fill=0.0, base=height - 1,
                                        pattern=above, channel_multiplier=-1).then_inc(masks_ready, 1)
            for s in range(2):
                nc.gpsimd.affine_select(out=g_sel[:, s, :, :, :], in_=g_sel[:, s, :, :, :],
                                        compare_op=ALU.not_equal, fill=1.0, base=0, pattern=[[-1, P]],
                                        channel_multiplier=1).then_inc(masks_ready, 1)
            nc.gpsimd.memset(row_ends[:, :, BB_COL - D:ROW - D], 0.0).then_inc(zeros_ready, 1)
            nc.gpsimd.memset(row_ends[:, GROUPS - 1, 0:P], 0.0).then_inc(zeros_ready, 1)

            def gather(k, slot, free=True):
                if free:
                    pool.wait_ge(g_ready, k - 1)
                    pool.wait_ge(up_ready, k - 1)
                nc.gpsimd.tensor_copy(rows_now[slot][:, :], rows[:, bass.ds(k, 1)]).then_inc(rows_now_ready, 1)
                pool.wait_ge(rows_now_ready, k + 1)
                pool.sem_inc(gather_issued, 1)
                nc.gpsimd.indirect_dma_start(out=gathered_rows[:, slot, :], out_offset=None, in_=by_rank_dram[:, :],
                                             in_offset=bass.IndirectOffsetOnAxis(ap=rows_now[slot][:, :], axis=0),
                                             ).then_inc(gathered[slot], 16)

            def up_low(k, slot):
                pool.wait_ge(up_hi_ready, k + 1)
                nc.gpsimd.tensor_tensor(out=up_rows[:, slot, LO, :], in0=gathered_rows[:, slot, 0:D],
                                        in1=up_rows[:, slot, HI, :], op=ALU.subtract).then_inc(up_ready, 1)

            def add_bias(k, pair, slot, free=True):
                pool.wait_ge(x_loaded[slot], pair * 16 + 16)
                if free:
                    pool.wait_ge(y_ready, k - 1)
                nc.gpsimd.tensor_tensor(out=xb[:, slot, :], in0=x_in[:, slot, :], in1=bias_all[:, :],
                                        op=ALU.add).then_inc(xb_ready, 1)

            def step(k, slot, next_pair):
                up_low(k, slot)
                gather(k + 2, slot)
                add_bias(k + 1, next_pair, 1 - slot)

            pool.wait_ge(bias_all_in, 16)
            pool.wait_ge(b1_in, 16)
            nc.gpsimd.tensor_tensor(out=bias_b1_terms[:, :], in0=b1_rows[:, :], in1=bias_all[:, :],
                                    op=ALU.mult).then_inc(bias_b1_step, 1)
            pool.wait_ge(ids_all_in, 32)
            nc.gpsimd.tensor_scalar(out=ids_all_f[:, :, :, :], in0=ids_all[:, :, :, :], scalar1=float(R), scalar2=None,
                                    op0=ALU.mult).then_inc(rows_step, 1)
            pool.wait_ge(masks_ready, 1)
            nc.gpsimd.tensor_copy(row_of_rank_f[:, :, :], row_of_rank[:, :, :]).then_inc(rows_step, 1)
            pool.wait_ge(rows_step, 2)
            for layer in (L0, L1):
                nc.gpsimd.tensor_tensor(
                    out=row_terms[:, :, layer, :], in0=ids_all_f[:, layer, :, :],
                    in1=row_of_rank_f[:, layer, :].unsqueeze(1).to_broadcast([P, NBLK, NB]),
                    op=ALU.add).then_inc(rows_step, 1)
            pool.wait_ge(rows_step, 4)
            for layer in (L0, L1):
                nc.gpsimd.tensor_tensor(
                    out=row_terms[:, :, layer, :], in0=row_terms[:, :, layer, :],
                    in1=rank_mask[:, layer, :].unsqueeze(1).to_broadcast([P, NBLK, NB]),
                    op=ALU.mult).then_inc(rows_step, 1)
            pool.wait_ge(rows_step, 6)
            nc.gpsimd.tensor_tensor(out=row_terms[:, :, L0, :], in0=row_terms[:, :, L0, :],
                                    in1=row_terms[:, :, L1, :], op=ALU.add).then_inc(rows_step, 1)
            pool.wait_ge(rows_step, 7)
            nc.gpsimd.tensor_tensor(out=row_terms[:, :, L0, 0:2], in0=row_terms[:, :, L0, 0:2],
                                    in1=row_terms[:, :, L0, 2:4], op=ALU.add).then_inc(rows_step, 1)
            pool.wait_ge(rows_step, 8)
            nc.gpsimd.tensor_tensor(out=row_sums[:, :].unsqueeze(2), in0=row_terms[:, :, L0, 0:1],
                                    in1=row_terms[:, :, L0, 1:2], op=ALU.add).then_inc(rows_step, 1)
            pool.wait_ge(rows_step, 9)
            nc.gpsimd.tensor_copy(rows[:, :], row_sums[:, :]).then_inc(rows_ready, 1)
            add_bias(0, 0, 0, free=False)
            pool.wait_ge(rows_ready, 1)
            pool.wait_ge(table_stored, (2 * C + 1) * 16)
            gather(0, 0, free=False)
            gather(1, 1, free=False)
            add_bias(1, 0, 1, free=False)
            up_low(0, 0)
            gather(2, 0)
            with pool.Fori(0, PAIRS - 2) as i:
                step(i * 2 + 1, 1, i + 1)
                step(i * 2 + 2, 0, i + 1)
            step(NBLK - 3, 1, PAIRS - 1)
            up_low(NBLK - 2, 0)
            add_bias(NBLK - 1, PAIRS - 1, 1)
            up_low(NBLK - 1, 1)

        def adapters_of(engine, k, layer):
            _, values = nc.values_load_multi_w_load_instructions(
                ids[0:1, bass.ds(k, 1), layer, :], engines=[engine.engine], min_val=0,
                max_val=(N0, N1)[layer] - 1,
                skip_runtime_bounds_check_because="the inputs index the adapter tables")
            return values

        @block.tensor
        def _(pe):
            def fill_room(f):
                if f >= FILL_BANKS:
                    wait_drained(pe, f - FILL_BANKS)

            pe.wait_ge(warm_ready, 1)
            for _ in range(WARM_UPS):
                nc.tensor.matmul(banks[XT][:, 0:P], warm[:, :], warm[:, :], start=True, stop=True)
            pe.wait_ge(ident_ready, 1)
            pe.wait_ge(bw_in, 16)
            for q in range(4):
                for r in range(4):
                    last = nc.tensor.transpose(bank(BW_FILL + q)[:, r * P:(r + 1) * P], bw_rows[:, :, 4 * q + r],
                                               ident[:, :])
                last.then_inc(filled, 1)
            pe.wait_ge(b1_in, 16)
            for c in range(C):
                last = nc.tensor.transpose(bank(B1_FILL)[:, c * P:(c + 1) * P], b1_rows[:, c * P:(c + 1) * P],
                                           ident[:, :])
            last.then_inc(filled, 1)

            def w_fills(chunks):
                for c in chunks:
                    fill_room(W_FILL[c])
                    if c % 2 == 0:
                        pe.wait_ge(w_in[c // 2], 16)
                    for oc in range(C):
                        last = nc.tensor.transpose(bank(W_FILL[c])[:, oc * P:(oc + 1) * P],
                                                   w_rows[:, oc, c * P:(c + 1) * P], ident[:, :])
                    last.then_inc(filled, 1)

            w_fills(range(C // 2))
            wait_drained(pe, B1_FILL)
            for g in range(4):
                for oc in range(C):
                    last = nc.tensor.matmul(bank(G_FILL)[:, g * P:(g + 1) * P], bw_cols[:, oc, g * P:(g + 1) * P],
                                            b1_cols[:, oc, :], start=(oc == 0), stop=(oc == C - 1))
            last.then_inc(filled, 1)
            w_fills(range(C // 2, C))

            def transpose_x(pair, slot):
                pe.wait_ge(x_loaded[slot], pair * 16 + 16)
                for c in range(C):
                    last = nc.tensor.transpose(banks[XT][:, c * P:(c + 1) * P], x_in[:, slot, c * P:(c + 1) * P],
                                               ident[:, :])
                last.then_inc(xt_filled, 1)

            transpose_x(0, 0)
            pe.wait_ge(a_in, 16)
            for g in range(4):
                fill_room(A_FILL + g)
                for c in range(C):
                    last = nc.tensor.transpose(bank(A_FILL + g)[:, c * P:(c + 1) * P],
                                               a_rows[:, g, c * P:(c + 1) * P], ident[:, :])
                last.then_inc(filled, 1)

            for h in range(2):
                fill_room(C1_FILL[h])
                for c in range(C // 2):
                    cols = slice((h * C // 2 + c) * P, (h * C // 2 + c + 1) * P)
                    for oc in range(C):
                        last = nc.tensor.matmul(bank(C1_FILL[h])[:, c * P:(c + 1) * P], w_rows[:, oc, cols],
                                                b1_cols[:, oc, :], start=(oc == 0), stop=(oc == C - 1))
                last.then_inc(filled, 1)

            HALVES = ((HI, HI), (HI, LO), (LO, HI))

            def base(k, slot, chunks, with_d=True, halves=range(2)):
                left = W_LEFT[slot]
                regions = [(left, left + HALF, P), (left, left + HALF, P + HALF)]
                if with_d:
                    at_bank, at = U_AT[slot]
                    start = min(at, left)
                    regions[at_bank] = (start, start + HALF + P, min(D_AT[slot], P + at_bank * HALF))
                for c in chunks:
                    for n, (x_part, w_part) in enumerate(HALVES):
                        for half in halves:
                            start, end, col = regions[half]
                            last = nc.tensor.matmul(psum[:, 2 * slot + half, start:end], xt[:, slot, c, x_part, :],
                                                    wd[:, w_part, c, col:col + end - start],
                                                    start=(c == 0 and n == 0), stop=(c == C - 1 and n == 2))
                if with_d and C - 1 in chunks and U_AT[slot][0] in halves:
                    last.then_inc(u_filled, 1)

            def edge_d(slot):
                for c in range(C):
                    for n, (x_part, d_part) in enumerate(HALVES):
                        last = nc.tensor.matmul(banks[EDGE_U][:, 0:P], xt[:, slot, c, x_part, :],
                                                wd[:, d_part, c, D_AT[slot]:D_AT[slot] + P],
                                                start=(c == 0 and n == 0), stop=(c == C - 1 and n == 2))
                last.then_inc(u_filled, 1)

            def wait_x(k):
                pe.wait_ge(xt_hi_ready, k + 1)
                pe.wait_ge(xt_lo_ready, k + 1)

            def wait_d(k):
                pe.wait_ge(sel0_ready, k + 1)
                pe.wait_ge(sel1_ready, k + 1)

            def add_gh(k, slot):
                pe.wait_ge(u_own_ready, k + 1)
                pe.wait_ge(g_ready, k + 1)
                nc.tensor.matmul(banks[U][:, 0:P], g_sel[:, slot, :, :, :], u_own[:, :],
                                 start=True, stop=True).then_inc(gh_filled, 1)

            def up(k, slot, by_half=False):
                pe.wait_ge(up_ready, k + 1)
                pe.wait_ge(u_ready, k + 1)
                for half in range(2):
                    for u_part, r_part in HALVES:
                        last = nc.tensor.matmul(products(slot)[:, half, :], u_sel[:, u_part, :],
                                                up_rows[:, slot, r_part, half * HALF:(half + 1) * HALF],
                                                start=False, stop=True, skip_group_check=True)
                    if half == 1 or by_half:
                        last.then_inc(out_filled, 1)

            def step(pair, slot, y_free=True):
                k = pair * 2 + slot
                wait_x(k)
                transpose_x(pair + slot, 1 - slot)
                wait_d(k)
                if y_free:
                    pe.wait_ge(y_ready, k - 1)
                base(k, slot, [0])
                add_gh(k - 1, 1 - slot)
                base(k, slot, range(1, C - 1))
                up(k - 1, 1 - slot)
                base(k, slot, [C - 1])

            wait_drained(pe, A_FILL + 1)
            wait_x(0)
            transpose_x(0, 1)
            base(0, 0, range(C), with_d=False)
            wait_d(0)
            edge_d(0)
            pe.wait_ge(masks_ready, 4)
            step(0, 1, y_free=False)
            with pe.Fori(1, PAIRS - 1) as i:
                step(i, 0)
                step(i, 1)
            step(PAIRS - 1, 0)
            wait_x(NBLK - 1)
            wait_d(NBLK - 1)
            pe.wait_ge(y_ready, NBLK - 2)
            d_half, other_half = U_AT[1][0], 1 - U_AT[1][0]
            base(NBLK - 1, 1, range(0, C // 2), halves=[d_half])
            add_gh(NBLK - 2, 0)
            base(NBLK - 1, 1, range(C // 2, C), halves=[d_half])
            base(NBLK - 1, 1, [0], halves=[other_half])
            up(NBLK - 2, 0)
            add_gh(NBLK - 1, 1)
            base(NBLK - 1, 1, range(1, C), halves=[other_half])
            up(NBLK - 1, 1, by_half=True)

        def by_adapter(fill, n):
            return bank(fill)[:, :].rearrange("p (c n r) -> p n c r", c=C, n=n)

        def by_rank(fill, n):
            return bank(fill)[:, :].rearrange("p (r n c) -> p c n r", n=n, c=C)

        def ranks_of_bw(q):
            return bw_cols[:, :, :].rearrange("p c (n r) -> p c n r", r=R)[:, :, :, 4 * q:4 * q + 4]

        def selected(slot, b, layer):
            col = D_AT[slot] + (b * 2 + layer) * R
            return wd[:, :, :, col:col + R]

        @block.scalar
        def _(act):
            def copy(dst, src):
                return nc.scalar.activation(dst, src, ACT.Copy)

            for q in (1, 3):
                act.wait_ge(filled, BW_FILL + q + 1)
                copy(ranks_of_bw(q), by_rank(BW_FILL + q, N0)).then_inc(act_drained, 1)
            act.wait_ge(bw_in, 16)
            copy(bw_by_rank[:, 0:R // 2, :], bw_rows[:, :, 0:R // 2].rearrange("p o r -> p r o")).then_inc(act_by_rank_ready, 1)

            def w_high(chunks):
                for c in chunks:
                    act.wait_ge(filled, W_FILL[c] + 1)
                    copy(wd[:, HI, c, P:P + D], bank(W_FILL[c])[:, :]).then_inc(act_drained, 1)

            w_high(range(C // 2))
            act.wait_ge(a1_in, 16)
            copy(a1_by_rank[:, 0:R // 2, :], a1_rows[:, :, 0:R // 2].rearrange("p o r -> p r o")).then_inc(act_by_rank_ready, 1)
            w_high(range(C // 2, C))

            def xt_high(k, slot, free=True):
                act.wait_ge(xt_filled, k + 1)
                if free:
                    act.wait_ge(u_filled, k - 1)
                copy(xt[:, slot, :, HI, :], banks[XT].rearrange("p (c m) -> p c m", c=C)).then_inc(xt_hi_ready, 1)

            def select(k, slot, n0, free=True):
                if free:
                    act.wait_ge(u_filled, k - 1)
                for b in range(NB):
                    last = copy(selected(slot, b, L0), table0_rounded[:, bass.ds(n0[b], 1), :, :, :])
                last.then_inc(sel0_ready, 1)

            def up_high(k, slot, pair, free=True):
                act.wait_ge(gathered[slot], pair * 16 + 16)
                if free:
                    act.wait_ge(u_filled, k)
                copy(up_rows[:, slot, HI, :], gathered_rows[:, slot, 0:D]).then_inc(up_hi_ready, 1)

            def u_high(k):
                act.wait_ge(gh_filled, k + 1)
                copy(u_sel[:, HI, :], banks[U][:, 0:P]).then_inc(u_hi_ready, 1)

            def step(k, slot, pair):
                up_high(k, slot, pair)
                xt_high(k + 1, 1 - slot)
                u_high(k - 1)
                select(k + 1, 1 - slot, adapters_of(act, k + 1, L0))

            act.wait_ge(ids_in, 32)
            xt_high(0, 0, free=False)
            for g in range(4):
                act.wait_ge(filled, A_FILL + g + 1)
                copy(table0_rounded[:, g * 8:g * 8 + 8, 0, :, :], by_adapter(A_FILL + g, 8)).then_inc(act_drained, 1)
            first_n0 = [adapters_of(act, s, L0) for s in range(2)]
            for h in range(2):
                act.wait_ge(c1_summed, h + 1)
                chunks = slice(h * C // 2, (h + 1) * C // 2)
                copy(table1_rounded[:, :, 0, chunks, :],
                     c1_sum[:, chunks, :].rearrange("p c (n r) -> p n c r", r=R)).then_inc(act_drained, 1)
            wait_drained(act, A_FILL + 3)
            select(0, 0, first_n0[0], free=False)
            xt_high(1, 1, free=False)
            select(1, 1, first_n0[1], free=False)
            up_high(0, 0, 0, free=False)
            with act.Fori(0, PAIRS - 1) as i:
                step(i * 2 + 1, 1, i)
                step(i * 2 + 2, 0, i + 1)
            up_high(NBLK - 1, 1, PAIRS - 1)
            u_high(NBLK - 2)
            u_high(NBLK - 1)

        @block.vector
        def _(dve):
            nc.vector.memset(warm[:, :], 0.0).then_inc(warm_ready, 1)

            def low(dst, whole, high):
                return nc.vector.tensor_tensor(out=dst, in0=whole, in1=high, op=ALU.subtract)

            for q in (0, 2):
                dve.wait_ge(filled, BW_FILL + q + 1)
                nc.vector.tensor_copy(ranks_of_bw(q), by_rank(BW_FILL + q, N0)).then_inc(dve_drained, 1)
            dve.wait_ge(filled, B1_FILL + 1)
            nc.vector.tensor_copy(b1_cols[:, :, :],
                                  bank(B1_FILL)[:, :].rearrange("p (c m) -> p c m", c=C)).then_inc(dve_drained, 1)
            dve.wait_ge(bw_in, 16)
            nc.vector.tensor_copy(bw_by_rank[:, R // 2:R, :],
                                  bw_rows[:, :, R // 2:R].rearrange("p o r -> p r o")).then_inc(dve_by_rank_ready, 1)

            def w_low(chunks):
                for c in chunks:
                    dve.wait_ge(act_drained, sum(g <= W_FILL[c] for g in BY_ACT))
                    low(wd[:, LO, c, P:P + D], bank(W_FILL[c])[:, :], wd[:, HI, c, P:P + D]).then_inc(dve_drained, 1)

            w_low(range(C // 2))
            dve.wait_ge(a1_in, 16)
            nc.vector.tensor_copy(a1_by_rank[:, R // 2:R, :],
                                  a1_rows[:, :, R // 2:R].rearrange("p o r -> p r o")).then_inc(dve_by_rank_ready, 1)
            dve.wait_ge(bias_b1_step, 1)
            dve.wait_ge(zeros_ready, 2)
            nc.vector.reduce_sum(row_ends[:, GROUPS - 1, BB_COL - D:BB_COL - D + 1], bias_b1_terms[:, :],
                                 axis=mybir.AxisListType.X).then_inc(bias_b1_ready, 1)
            dve.wait_ge(filled, G_FILL + 1)
            nc.vector.tensor_copy(row_ends[:, 0:N0 * R // P, 0:P],
                                  bank(G_FILL)[:, :].rearrange("p (g m) -> p g m", m=P)).then_inc(dve_drained, 1)
            w_low(range(C // 2, C))

            def xt_low(k, slot):
                dve.wait_ge(xt_hi_ready, k + 1)
                low(xt[:, slot, :, LO, :], banks[XT].rearrange("p (c m) -> p c m", c=C),
                    xt[:, slot, :, HI, :]).then_inc(xt_lo_ready, 1)

            def select(k, slot, n1, free=True):
                if free:
                    dve.wait_ge(u_filled, k - 1)
                for b in range(NB):
                    last = nc.vector.tensor_copy(selected(slot, b, L1), table1_rounded[:, bass.ds(n1[b], 1), :, :, :])
                last.then_inc(sel1_ready, 1)

            def select_g(slot, n1, pair):
                dve.wait_ge(gathered[slot], pair * 16 + 16)
                nc.vector.tensor_copy(bb_sel[:, slot, :], gathered_rows[:, slot, BB_COL:BB_COL + 1])
                for b in range(NB):
                    ranks = slice(2 * R * b, 2 * R * b + R)
                    last = nc.vector.tensor_copy(g_sel[ranks, slot, b, L1, :],
                                                 gathered_rows[ranks, slot, bass.ds(n1[b] * R + G_COL, R)])
                last.then_inc(g_ready, 1)

            def transpose_u(k, slot, source):
                dve.wait_ge(u_filled, k + 1)
                nc.vector.transpose(out=u_blocks[:, :], in_=source).then_inc(u_blocks_ready, 1)
                dve.wait_ge(u_blocks_ready, k + 1)
                dve.wait_ge(g_ready, k + 1)
                nc.vector.scalar_tensor_tensor(out=u_own[:, :], in0=u_blocks[:, :], scalar=bb_sel[:, slot, :],
                                               in1=batch_mask[:, :, :].rearrange("p b s -> p (b s)"),
                                               op0=ALU.add, op1=ALU.mult).then_inc(u_own_ready, 1)

            def u_split(k):
                dve.wait_ge(u_hi_ready, k + 1)
                low(u_sel[:, LO, :], banks[U][:, 0:P], u_sel[:, HI, :]).then_inc(u_ready, 1)

            def finish(k, pair, slot, stored=True):
                dve.wait_ge(out_filled, k + 1)
                dve.wait_ge(xb_ready, k + 1)
                if stored:
                    dve.wait_ge(y_stored[slot], pair * 16)
                nc.vector.tensor_tensor(out=y[:, slot, :].rearrange("p (h n) -> p h n", h=2), in0=products(slot),
                                        in1=xb[:, slot, :].rearrange("p (h n) -> p h n", h=2),
                                        op=ALU.add).then_inc(y_ready, 1)

            def step(k, slot, last_pair, next_pair, stored=True, deferred_g=None, first=False):
                transpose_u(k - 1, 1 - slot, banks[EDGE_U][:, 0:P] if first else u_of(1 - slot))
                xt_low(k + 1, 1 - slot)
                n1 = adapters_of(dve, k + 1, L1)
                next_g = (1 - slot, n1, next_pair)
                u_split(k - 1)
                if deferred_g is not None:
                    select_g(*deferred_g)
                select(k + 1, 1 - slot, n1)
                if not first:
                    select_g(*next_g)
                finish(k - 1, last_pair, 1 - slot, stored)
                return next_g

            xt_low(0, 0)
            for g in range(4):
                dve.wait_ge(act_drained, sum(h <= A_FILL + g for h in BY_ACT))
                low(table0_rounded[:, g * 8:g * 8 + 8, 1, :, :], by_adapter(A_FILL + g, 8),
                    table0_rounded[:, g * 8:g * 8 + 8, 0, :, :]).then_inc(dve_drained, 1)
            dve.wait_ge(ids_in, 32)
            first_n1 = [adapters_of(dve, s, L1) for s in range(2)]
            for h in range(2):
                chunks = slice(h * C // 2, (h + 1) * C // 2)
                dve.wait_ge(filled, C1_FILL[h] + 1)
                nc.vector.tensor_tensor(out=c1_sum[:, chunks, :],
                                        in0=bank(C1_FILL[h])[:, 0:D // 2].rearrange("p (c m) -> p c m", c=C // 2),
                                        in1=b1_cols[:, chunks, :], op=ALU.add).then_inc(c1_summed, 1)
                dve.wait_ge(c1_summed, h + 1)
                dve.wait_ge(act_drained, sum(g <= C1_FILL[h] for g in BY_ACT))
                low(table1_rounded[:, :, 1, chunks, :], c1_sum[:, chunks, :].rearrange("p c (n r) -> p n c r", r=R),
                    table1_rounded[:, :, 0, chunks, :]).then_inc(dve_drained, 1)
            wait_drained(dve, C1_FILL[1])
            select(0, 0, first_n1[0], free=False)
            xt_low(1, 1)
            select(1, 1, first_n1[1], free=False)
            select_g(0, first_n1[0], 0)
            third_g = step(1, 1, 0, 1, stored=False, deferred_g=(1, first_n1[1], 0), first=True)
            step(2, 0, 0, 1, stored=False, deferred_g=third_g)
            with dve.Fori(1, PAIRS - 1) as i:
                step(i * 2 + 1, 1, i, i + 1)
                step(i * 2 + 2, 0, i, i + 1)
            transpose_u(NBLK - 2, 0, u_of(0))
            u_split(NBLK - 2)
            dve.wait_ge(gh_filled, NBLK - 1)
            transpose_u(NBLK - 1, 1, u_of(1))
            finish(NBLK - 2, PAIRS - 1, 0)
            u_split(NBLK - 1)
            dve.wait_ge(xb_ready, NBLK)
            dve.wait_ge(y_stored[1], (PAIRS - 1) * 16)
            for half in range(2):
                cols = slice(half * HALF, (half + 1) * HALF)
                dve.wait_ge(out_filled, NBLK + half)
                nc.vector.tensor_tensor(out=y[:, 1, cols], in0=products(1)[:, half, :], in1=xb[:, 1, cols],
                                        op=ALU.add).then_inc(y_ready, 1)


_INPUTS = ["x", "itok_B_6_15", "itok_B_3_7", "L0_cond_base_weight", "L0_cond_base_bias",
           "L0_cond_lora_A_w", "L0_cond_lora_B_w", "L1_cond_A", "L1_cond_B"]


def kernel(**inputs):
    import numpy as np
    import concourse.bacc as bacc
    from concourse.bass_utils import run_bass_kernel_spmd

    nc = bacc.Bacc("TRN2", target_bir_lowering=False, num_devices=1)
    arrays, args = {}, []
    for name in _INPUTS:
        a = np.ascontiguousarray(inputs[name])
        arrays[f"in_{name}"] = a
        args.append(nc.dram_tensor(f"in_{name}", a.shape, mybir.dt.from_np(a.dtype), kind="ExternalInput").ap())
    out = nc.dram_tensor("out", (B, S, D), F32, kind="ExternalOutput").ap()
    two_lora_layers(nc, *args, out)
    return run_bass_kernel_spmd(nc, [arrays], core_ids=[0]).results[0]["out"]
```
